# Optimizing a Trainium2 kernel written in Bass

```python
import numpy as np
import jax
import jax.numpy as jnp

def _softmax(x, axis=-1):
    return jax.nn.softmax(x, axis=axis)

def _gelu(x):
    return jax.nn.gelu(x, approximate=True)

def _silu(x):
    return jax.nn.silu(x)

def _sigmoid(x):
    return jax.nn.sigmoid(x)

def _layernorm(x, axis=-1, eps=1e-05):
    m = jnp.mean(x, axis=axis, keepdims=True)
    v = jnp.var(x, axis=axis, keepdims=True)
    return (x - m) / jnp.sqrt(v + eps)

def _scatter_add(tgt, idx, src, axis=0):
    return tgt.at[idx].add(src)

def _segment_sum(src, seg, n):
    return jax.ops.segment_sum(src, seg, n)
kernel_name = 'mk_adj_seq_d1_adj_r2_26f61b'

def setup_inputs(seed: int=0):
    np.random.seed(seed)
    _w = jnp.asarray

    def _rec_inputs():
        import jax
        import jax.numpy as jnp
        _gk = jax.random.key(seed)
        x = -0.0005207 + 1.001 * jax.random.normal(jax.random.fold_in(_gk, 1), (4096, 256), jnp.float32)
        _w = (1.0 + jnp.arange(4096, dtype=jnp.float32)) ** (-0.5)
        _w = _w / _w.mean()
        _pij = jnp.clip(0.000488281 * _w[:, None] * _w[None, :], 0.0, 1.0)
        _a = jax.random.uniform(jax.random.fold_in(_gk, 2), (4096, 4096)) < _pij
        adj = _a.astype(jnp.int32)
        return (x, adj)
    x, adj = _rec_inputs()

    def _L0_gnn_setup():
        import jax, jax.numpy as jnp
        import numpy as np
        D_MODEL = 256
        N_HEADS = 8
        D_K = D_MODEL // N_HEADS
        D_FF = 1024
        N = 2048
        EPS = 1e-05

        def _layer_norm(x, g, b):
            mu = jnp.mean(x, axis=-1, keepdims=True)
            var = jnp.mean(jnp.square(x - mu), axis=-1, keepdims=True)
            return (x - mu) * jax.lax.rsqrt(var + EPS) * g + b
        key = jax.random.key(seed)
        ks = jax.random.split(key, 16)
        s = 1.0 / np.sqrt(D_MODEL)
        sf = 1.0 / np.sqrt(D_FF)
        inp = {'h': jax.random.normal(ks[0], (N, D_MODEL), dtype=jnp.float32), 'adj': jax.random.randint(ks[1], (N, N), 0, 2, dtype=jnp.int32), 'Wq': jax.random.uniform(ks[2], (D_MODEL, D_MODEL), jnp.float32, -s, s), 'bq': jnp.zeros((D_MODEL,), jnp.float32), 'Wk': jax.random.uniform(ks[3], (D_MODEL, D_MODEL), jnp.float32, -s, s), 'bk': jnp.zeros((D_MODEL,), jnp.float32), 'Wv': jax.random.uniform(ks[4], (D_MODEL, D_MODEL), jnp.float32, -s, s), 'bv': jnp.zeros((D_MODEL,), jnp.float32), 'Wo': jax.random.uniform(ks[5], (D_MODEL, D_MODEL), jnp.float32, -s, s), 'bo': jnp.zeros((D_MODEL,), jnp.float32), 'W1': jax.random.uniform(ks[6], (D_FF, D_MODEL), jnp.float32, -s, s), 'b1': jnp.zeros((D_FF,), jnp.float32), 'W2': jax.random.uniform(ks[7], (D_MODEL, D_FF), jnp.float32, -sf, sf), 'b2': jnp.zeros((D_MODEL,), jnp.float32), 'ln1_g': jnp.ones((D_MODEL,), jnp.float32), 'ln1_b': jnp.zeros((D_MODEL,), jnp.float32), 'ln2_g': jnp.ones((D_MODEL,), jnp.float32), 'ln2_b': jnp.zeros((D_MODEL,), jnp.float32)}
        return inp
    _L0_gnn_all = _L0_gnn_setup()
    _L0_gnn_in = {k: v for k, v in _L0_gnn_all.items() if k in ('Wq', 'bq', 'Wk', 'bk', 'Wv', 'bv', 'Wo', 'bo', 'W1', 'b1', 'W2', 'b2', 'ln1_g', 'ln1_b', 'ln2_g', 'ln2_b')}
    del _L0_gnn_all
    return {'x': x, 'adj': adj, 'L0_gnn_Wq': _L0_gnn_in['Wq'], 'L0_gnn_bq': _L0_gnn_in['bq'], 'L0_gnn_Wk': _L0_gnn_in['Wk'], 'L0_gnn_bk': _L0_gnn_in['bk'], 'L0_gnn_Wv': _L0_gnn_in['Wv'], 'L0_gnn_bv': _L0_gnn_in['bv'], 'L0_gnn_Wo': _L0_gnn_in['Wo'], 'L0_gnn_bo': _L0_gnn_in['bo'], 'L0_gnn_W1': _L0_gnn_in['W1'], 'L0_gnn_b1': _L0_gnn_in['b1'], 'L0_gnn_W2': _L0_gnn_in['W2'], 'L0_gnn_b2': _L0_gnn_in['b2'], 'L0_gnn_ln1_g': _L0_gnn_in['ln1_g'], 'L0_gnn_ln1_b': _L0_gnn_in['ln1_b'], 'L0_gnn_ln2_g': _L0_gnn_in['ln2_g'], 'L0_gnn_ln2_b': _L0_gnn_in['ln2_b']}

def reference(x, adj, L0_gnn_Wq, L0_gnn_bq, L0_gnn_Wk, L0_gnn_bk, L0_gnn_Wv, L0_gnn_bv, L0_gnn_Wo, L0_gnn_bo, L0_gnn_W1, L0_gnn_b1, L0_gnn_W2, L0_gnn_b2, L0_gnn_ln1_g, L0_gnn_ln1_b, L0_gnn_ln2_g, L0_gnn_ln2_b):
    import jax
    import jax.numpy as jnp

    def _L0_gnn_ref(h, adj, Wq, bq, Wk, bk, Wv, bv, Wo, bo, W1, b1, W2, b2, ln1_g, ln1_b, ln2_g, ln2_b):
        import jax, jax.numpy as jnp
        import numpy as np
        D_MODEL = 256
        N_HEADS = 8
        D_K = D_MODEL // N_HEADS
        D_FF = 1024
        N = 2048
        EPS = 1e-05

        def _layer_norm(x, g, b):
            mu = jnp.mean(x, axis=-1, keepdims=True)
            var = jnp.mean(jnp.square(x - mu), axis=-1, keepdims=True)
            return (x - mu) * jax.lax.rsqrt(var + EPS) * g + b
        n = h.shape[0]
        mask = adj.astype(jnp.float32) + jnp.eye(n, dtype=jnp.float32)
        q = (h @ Wq.T + bq).reshape(n, N_HEADS, D_K)
        k = (h @ Wk.T + bk).reshape(n, N_HEADS, D_K)
        v = (h @ Wv.T + bv).reshape(n, N_HEADS, D_K)
        scores = jnp.einsum('nhd,mhd->hnm', q, k) / jnp.sqrt(jnp.float32(D_K))
        scores = jnp.where(mask[None, :, :] == 0, jnp.float32(-1000000000.0), scores)
        attn = jax.nn.softmax(scores, axis=-1)
        ctx = jnp.einsum('hnm,mhd->nhd', attn, v).reshape(n, D_MODEL)
        attn_out = ctx @ Wo.T + bo
        h1 = _layer_norm(h + attn_out, ln1_g, ln1_b)
        ff = jax.nn.relu(h1 @ W1.T + b1) @ W2.T + b2
        h2 = _layer_norm(h1 + ff, ln2_g, ln2_b)
        return h2
    x = _L0_gnn_ref(x, adj, L0_gnn_Wq, L0_gnn_bq, L0_gnn_Wk, L0_gnn_bk, L0_gnn_Wv, L0_gnn_bv, L0_gnn_Wo, L0_gnn_bo, L0_gnn_W1, L0_gnn_b1, L0_gnn_W2, L0_gnn_b2, L0_gnn_ln1_g, L0_gnn_ln1_b, L0_gnn_ln2_g, L0_gnn_ln2_b)
    return x

_drawn_inputs = setup_inputs


def setup_inputs(seed=0):
    import zlib

    import numpy as np

    out = dict(_drawn_inputs(seed))
    spreads = {'L0_gnn_bq': (0.0, 0.8),
     'L0_gnn_bk': (0.0, 0.8),
     'L0_gnn_bv': (0.0, 0.1),
     'L0_gnn_bo': (0.0, 0.1),
     'L0_gnn_b1': (0.0, 0.1),
     'L0_gnn_b2': (0.0, 0.1),
     'L0_gnn_ln1_g': (1.0, 0.2),
     'L0_gnn_ln1_b': (0.0, 0.1),
     'L0_gnn_ln2_g': (1.0, 0.2),
     'L0_gnn_ln2_b': (0.0, 0.1)}
    factors = {}
    for name, (base, spread) in spreads.items():
        noise = np.random.default_rng([zlib.crc32(name.encode()), seed]).standard_normal(out[name].shape)
        drawn = base * np.exp(spread * noise) if base else spread * noise
        out[name] = jnp.asarray(drawn.astype(out[name].dtype))
    for name, factor in factors.items():
        out[name] = (out[name] * factor).astype(out[name].dtype)
    return out
```

```python
from contextlib import ExitStack

import concourse.bass as bass
from concourse import mybir

ALU = mybir.AluOpType
ACT = mybir.ActivationFunctionType
F32 = mybir.dt.float32
I32 = mybir.dt.int32
AX_X = mybir.AxisListType.X

P = 128
N = 4096
D = 256
HEADS = 8
DK = D // HEADS
FF = 1024
EPS = 1e-5
TILES = N // P
GROUP = 4
GROUPS = TILES // GROUP
KC = D // P
FC = FF // P
SCALE = 1.0 / float(DK) ** 0.5
NEG = -1.0e9
BANK = 512
BANKS = 8


def build(nc, x, xT, adj, wqkvT, bq, bk, bqkv, woT, bo, w1T, b1, w2T, b2, g1, be1, g2, be2, out):
    with ExitStack() as ctx:
        def sb(name, shape, dt=F32):
            return ctx.enter_context(nc.sbuf_tensor(name, shape, dt))

        def sem(name):
            return ctx.enter_context(nc.semaphore(name))

        ps = ctx.enter_context(nc.psum_tensor("ps", [P, BANKS, BANK], F32))

        wqkv = sb("wqkv", [P, KC, 3 * D])
        wo = sb("wo", [P, KC, D])
        w1 = sb("w1", [P, KC, FF])
        w2 = sb("w2", [P, FC, D])
        bias_qkv = sb("bias_qkv", [P, 3 * D])
        bias_qT = sb("bias_qT", [P, KC])
        bias_kT = sb("bias_kT", [P, KC])
        bias_1T = sb("bias_1T", [P, FC])
        rows = {n: sb("row_" + n, [P, D]) for n in ("bo", "b2", "g1", "be1", "g2", "be2")}
        ident = sb("ident", [P, P])
        neg_half = sb("neg_half", [P, GROUP])
        eps_col = sb("eps_col", [P, GROUP])
        CONSTS = 4

        kv_all = sb("kv_all", [P, TILES, 2 * D])

        s_const = sem("s_const")
        s_weights = sem("s_weights")

        xbuf = sb("xbuf", [P, 2, KC, GROUP * P])
        s_x = [sem("s_x0"), sem("s_x1")]
        s_qkv_ps = sem("s_qkv_ps")
        s_qkv_raw = sem("s_qkv_raw")
        s_qkv = sem("s_qkv")

        gXT = sb("gXT", [P, 1, KC, GROUP * P])
        gKT = sb("gKT", [P, KC, N])
        gQT = sb("gQT", [P, KC, P])
        gx = sb("gx", [P, 2, KC, P])
        gadj = sb("gadj", [P, N], I32)
        gmask = sb("gmask", [P, N])
        gS = sb("gS", [P, N])
        gPT = sb("gPT", [P, 8 * P])
        gstat = sb("gstat", [P, 4])

        def post_stage(name, g):
            shapes = {
                "ctx": [P, g, D], "ctxT": [P, KC, g * P], "x": [P, g, D], "h1": [P, g, D], "ffT": [P, FC, g * P],
                "stats": [P, g, 6], "mv": [P, g, 2], "rstd": [P, g], "spare": [P, 1],
            }
            signals = ("x_loaded x_biased ctxT_ps ctxT_done attn_ps res1 mv1 rstd1 norm1 h1_done h1T_ps h1T "
                       "ff_ps ff h1_b2 out_ps res2 mv2 rstd2 norm2 final stored link plink").split()
            return {"g": g, **{n: sb(name + n, s) for n, s in shapes.items()}, **{n: sem(name + n) for n in signals}}

        post = post_stage("g_", 1)

        s_gx = sem("s_gx")
        s_gkt_ps = sem("s_gkt_ps")
        s_gkt = sem("s_gkt")
        s_gadj = sem("s_gadj")
        s_gmask = sem("s_gmask")
        s_gdiag = sem("s_gdiag")
        s_gxq = sem("s_gxq")
        s_gqt_ps = sem("s_gqt_ps")
        s_gqt = sem("s_gqt")
        s_gscores = sem("s_gscores")
        s_gmasked = sem("s_gmasked")
        s_gmax = sem("s_gmax")
        s_gnm = sem("s_gnm")
        s_gprobs = sem("s_gprobs")
        s_gpt_ps = sem("s_gpt_ps")
        s_gpt = sem("s_gpt")
        s_gpv = sem("s_gpv")
        s_grl = sem("s_grl")
        s_gctx = sem("s_gctx")
        s_kv_out = sem("s_kv_out")

        WEIGHT_DMAS = 8 + len(rows)
        PT_TILES = 8
        PT_PARTS = TILES // PT_TILES

        block = ctx.enter_context(nc.Block())

        def post_sync(sp, q, n, t):
            sp.wait_ge(q["res1"], n)
            sp.dma_start(q["x"][:], x.rearrange("(t p) d -> p t d", p=P)[:, bass.ds(t * q["g"], q["g"]), :]).then_inc(q["x_loaded"], 16)

        def post_store(sp, q, n, t):
            sp.wait_ge(q["final"], n + 1)
            sp.dma_start(out.rearrange("(t p) d -> p t d", p=P)[:, bass.ds(t * q["g"], q["g"]), :], q["h1"][:]).then_inc(q["stored"], 16)

        def transposed(pe, src, g, bank, done):
            for k in range(KC):
                for j in range(g):
                    c = (k * g + j) * P
                    last = nc.tensor.transpose(ps[:, bank + c // BANK, c % BANK:c % BANK + P],
                                               src[:, j, k * P:(k + 1) * P], ident[:])
            last.then_inc(done, 1)

        def post_pe(pe, q, n, bank, ctx_sem, ctx_value):
            g = q["g"]
            pe.wait_ge(ctx_sem, ctx_value)
            transposed(pe, q["ctx"], g, bank, q["ctxT_ps"])
            pe.wait_ge(q["ctxT_done"], n + 1)
            for j in range(g):
                for k in range(KC):
                    last = nc.tensor.matmul(ps[:, bank + 2 + j * D // BANK, j * D % BANK:j * D % BANK + D],
                                            q["ctxT"][:, k, j * P:(j + 1) * P], wo[:, k, :],
                                            start=(k == 0), stop=(k == KC - 1))
            last.then_inc(q["attn_ps"], 1)
            pe.wait_ge(q["h1_done"], n + 1)
            transposed(pe, q["h1"], g, bank, q["h1T_ps"])
            pe.wait_ge(q["h1T"], n + 1)
            for f in range(FC):
                if f >= 2:
                    pe.wait_ge(q["ff"], n * FC + f - 1)
                for k in range(KC):
                    last = nc.tensor.matmul(ps[:, bank + f % 2, 0:g * P], w1[:, k, f * P:(f + 1) * P],
                                            q["ctxT"][:, k, :], start=(k == 0), stop=(k == KC - 1))
                last.then_inc(q["ff_ps"], 1)
            pe.wait_ge(q["ff"], n * FC + FC)
            for j in range(g):
                for f in range(FC):
                    last = nc.tensor.matmul(ps[:, bank + 2 + j * D // BANK, j * D % BANK:j * D % BANK + D],
                                            q["ffT"][:, f, j * P:(j + 1) * P], w2[:, f, :],
                                            start=(f == 0), stop=(f == FC - 1))
            last.then_inc(q["out_ps"], 1)

        def flat(ap):
            return ap.rearrange("p a b -> p (a b)")

        def post_act(act, q, n, bank):
            g = q["g"]
            w = KC * g * P
            for ready, done in ((q["ctxT_ps"], q["ctxT_done"]), (q["h1T_ps"], q["h1T"])):
                act.wait_ge(ready, n + 1)
                src = ps[:, bank:bank + (w + BANK - 1) // BANK, :].rearrange("p a b -> p (a b)")[:, 0:w]
                nc.scalar.copy(flat(q["ctxT"][:]), src).then_inc(done, 1)
            for f in range(FC):
                act.wait_ge(q["ff_ps"], n * FC + f + 1)
                nc.scalar.activation(q["ffT"][:, f, :], ps[:, bank + f % 2, 0:g * P], ACT.Relu,
                                     bias=bias_1T[:, f:f + 1]).then_inc(q["ff"], 1)

        def post_dve(dve, q, n, bank):
            g = q["g"]
            w = g * D
            src = ps[:, bank + 2:bank + 2 + (w + BANK - 1) // BANK, :].rearrange("p a b -> p (a b)")[:, 0:w]
            for ps_ready, other, dst, res, mv_done, rstd_ready, norm in (
                    (q["attn_ps"], q["x_biased"], q["x"], q["res1"], q["mv1"], q["rstd1"], q["norm1"]),
                    (q["out_ps"], q["h1_b2"], q["h1"], q["res2"], q["mv2"], q["rstd2"], q["norm2"])):
                dve.wait_ge(ps_ready, n + 1)
                dve.wait_ge(other, n + 1)
                nc.vector.tensor_tensor(flat(q["h1"][:]), src, flat(dst[:]), ALU.add).then_inc(res, 1)
                dve.wait_ge(res, n + 1)
                for j in range(g):
                    last = nc.vector.bn_stats(q["stats"][:, j, :], q["h1"][:, j, :])
                last.then_inc(q["link"], 1)
                dve.wait_ge(q["link"], n * 2 + (2 if norm is q["norm2"] else 1))
                nc.vector.memset(q["spare"][:], 0.0)
                for j in range(g):
                    last = nc.vector.bn_aggr(q["mv"][:, j, :], q["stats"][:, j, :])
                last.then_inc(mv_done, 1)
                dve.wait_ge(rstd_ready, n + 1)
                for j in range(g):
                    last = nc.vector.tensor_scalar(q["h1"][:, j, :], q["h1"][:, j, :], q["mv"][:, j, 0:1],
                                                   q["rstd"][:, j:j + 1], ALU.subtract, ALU.mult)
                last.then_inc(norm, 1)

        def wide(ap, g):
            return ap[:].unsqueeze(1).to_broadcast([P, g, D])

        def post_pool(pool, q, n):
            g = q["g"]
            pool.wait_ge(q["x_loaded"], (n + 1) * 16)
            nc.gpsimd.tensor_tensor(q["x"][:], q["x"][:], wide(rows["bo"], g), ALU.add).then_inc(q["x_biased"], 1)
            for mv, rstd, norm, gain, shift, done, k in ((q["mv1"], q["rstd1"], q["norm1"], "g1", "be1", q["h1_done"], 0),
                                                        (q["mv2"], q["rstd2"], q["norm2"], "g2", "be2", q["final"], 1)):
                pool.wait_ge(mv, n + 1)
                nc.gpsimd.tensor_tensor(q["rstd"][:], q["mv"][:, :, 1], eps_col[:, 0:g], ALU.add).then_inc(q["plink"], 1)
                pool.wait_ge(q["plink"], n * 4 + 2 * k + 1)
                nc.gpsimd.tensor_tensor(q["rstd"][:], q["rstd"][:], neg_half[:, 0:g], ALU.pow).then_inc(rstd, 1)
                pool.wait_ge(norm, n + 1)
                nc.gpsimd.tensor_tensor(q["h1"][:], q["h1"][:], wide(rows[gain], g), ALU.mult).then_inc(q["plink"], 1)
                pool.wait_ge(q["plink"], n * 4 + 2 * k + 2)
                nc.gpsimd.tensor_tensor(q["h1"][:], q["h1"][:], wide(rows[shift], g), ALU.add).then_inc(done, 1)
                if k == 0:
                    pool.wait_ge(q["h1T_ps"], n + 1)
                    nc.gpsimd.tensor_tensor(q["h1"][:], q["h1"][:], wide(rows["b2"], g), ALU.add).then_inc(q["h1_b2"], 1)

        @block.sync
        def _(sp):
            with sp.Fori(0, GROUPS // 2) as i:
                for j in range(2):
                    sp.wait_ge(s_qkv_raw, i * 2 * GROUP)
                    sp.dma_start(xbuf[:, j], xT.rearrange("(k p) n -> p k n", p=P)[:, :, bass.ds((i * 2 + j) * GROUP * P, GROUP * P)]
                                 ).then_inc(s_x[j], 16)
            with sp.Fori(0, GROUPS) as c:
                sp.wait_ge(s_gkt, c * KC)
                sp.dma_start(gXT[:, 0], xT.rearrange("(k p) n -> p k n", p=P)[:, :, bass.ds(c * GROUP * P, GROUP * P)]).then_inc(s_gx, 16)
            with sp.Fori(0, TILES) as t:
                sp.wait_ge(s_gqt_ps, t)
                sp.dma_start(gx[:, 0], xT.rearrange("(k p) n -> p k n", p=P)[:, :, bass.ds(t * P, P)]).then_inc(s_gxq, 16)
                sp.wait_ge(s_gmask, t)
                sp.dma_start(gadj[:], adj[bass.ds(t * P, P), :]).then_inc(s_gadj, 16)
                sp.wait_ge(post["stored"], t * 16)
                post_sync(sp, post, t, t)
                post_store(sp, post, t, t)
            sp.wait_ge(post["stored"], TILES * 16)

        @block.gpsimd
        def _(pool):
            nc.gpsimd.memset(ident[:], 0.0).then_inc(s_const, 1)
            nc.gpsimd.memset(neg_half[:], -0.5).then_inc(s_const, 1)
            nc.gpsimd.memset(eps_col[:], EPS).then_inc(s_const, 1)
            pool.wait_ge(s_const, 3)
            nc.gpsimd.affine_select(out=ident[:], in_=ident[:], compare_op=ALU.not_equal, fill=1.0, base=0,
                                    pattern=[[-1, P]], channel_multiplier=1).then_inc(s_const, 1)
            pool.wait_ge(s_const, CONSTS)
            pool.wait_ge(s_weights, 16 * WEIGHT_DMAS)
            with pool.Fori(0, TILES) as t:
                pool.wait_ge(s_qkv_raw, t + 1)
                nc.gpsimd.tensor_tensor(kv_all[:, bass.ds(t, 1), :], kv_all[:, bass.ds(t, 1), :],
                                        bias_qkv[:, D:3 * D].unsqueeze(1), ALU.add).then_inc(s_qkv, 1)
            with pool.Fori(0, TILES) as t:
                post_pool(pool, post, t)

        @block.scalar
        def _(act):
            for dst, src in ((wqkv, wqkvT.rearrange("(k p) n -> p k n", p=P)), (wo, woT.rearrange("(k p) n -> p k n", p=P)),
                             (w1, w1T.rearrange("(k p) n -> p k n", p=P)), (w2, w2T.rearrange("(k p) n -> p k n", p=P)),
                             (bias_qT, bq), (bias_kT, bk), (bias_1T, b1),
                             (bias_qkv, bqkv.to_broadcast([P, 3 * D]))):
                act.dma_start(dst[:], src).then_inc(s_weights, 16)
            for name, src in (("bo", bo), ("b2", b2), ("g1", g1), ("be1", be1), ("g2", g2), ("be2", be2)):
                act.dma_start(rows[name][:], src.to_broadcast([P, D])).then_inc(s_weights, 16)
            act.wait_ge(s_weights, 16 * WEIGHT_DMAS)
            with act.Fori(0, TILES) as t:
                act.wait_ge(s_qkv_ps, t + 1)
                nc.scalar.copy(kv_all[:, bass.ds(t, 1), :], ps[:, 0:1, :]).then_inc(s_qkv_raw, 1)
            with act.Fori(0, GROUPS) as c:
                for half in range(KC):
                    act.wait_ge(s_gkt_ps, c * KC + half + 1)
                    nc.scalar.activation(gKT[:, half, bass.ds(c * GROUP * P, GROUP * P)], ps[:, half, :], ACT.Identity,
                                         bias=bias_kT[:, half:half + 1]).then_inc(s_gkt, 1)
            with act.Fori(0, TILES) as t:
                act.wait_ge(s_gqt_ps, t + 1)
                for half in range(KC):
                    last = nc.scalar.activation(gQT[:, half, :], ps[:, 0, half * P:(half + 1) * P], ACT.Identity,
                                                bias=bias_qT[:, half:half + 1])
                last.then_inc(s_gqt, 1)
                for h in range(HEADS):
                    n = t * HEADS + h
                    act.wait_ge(s_gnm, n + 1)
                    nc.scalar.activation(gS[:], gS[:], ACT.Exp, bias=gstat[:, 1:2], scale=SCALE,
                                         accum_out=gstat[:, 2:3]).then_inc(s_gprobs, 1)
                    for part in range(PT_PARTS):
                        act.wait_ge(s_gpt_ps, n * PT_PARTS + part + 1)
                        nc.scalar.copy(gPT[:], flat(ps[:, 0:PT_TILES * P // BANK, :])).then_inc(s_gpt, 1)
                post_act(act, post, t, 0)

        @block.tensor
        def _(pe):
            pe.wait_ge(s_weights, 16 * WEIGHT_DMAS)
            pe.wait_ge(s_const, CONSTS)
            with pe.Fori(0, GROUPS // 2) as i:
                for j in range(2):
                    pe.wait_ge(s_x[j], (i + 1) * 16)
                    for r in range(GROUP):
                        n = (i * 2 + j) * GROUP + r
                        pe.wait_ge(s_qkv_raw, n)
                        for k in range(KC):
                            last = nc.tensor.matmul(ps[:, 0, :], xbuf[:, j, k, r * P:(r + 1) * P], wqkv[:, k, D:3 * D],
                                                    start=(k == 0), stop=(k == KC - 1))
                        last.then_inc(s_qkv_ps, 1)
            pe.wait_ge(s_qkv_raw, TILES)
            with pe.Fori(0, GROUPS) as c:
                pe.wait_ge(s_gx, (c + 1) * 16)
                pe.wait_ge(s_gkt, c * KC)
                for half in range(KC):
                    for k in range(KC):
                        last = nc.tensor.matmul(ps[:, half, :], wqkv[:, k, D + half * P:D + (half + 1) * P], gXT[:, 0, k, :],
                                                start=(k == 0), stop=(k == KC - 1))
                    last.then_inc(s_gkt_ps, 1)
            pe.wait_ge(s_gkt, GROUPS * KC)
            pe.wait_ge(s_qkv, TILES)
            with pe.Fori(0, TILES) as t:
                pe.wait_ge(post["res2"], t)
                pe.wait_ge(s_gxq, (t + 1) * 16)
                for half in range(KC):
                    for k in range(KC):
                        last = nc.tensor.matmul(ps[:, 0, half * P:(half + 1) * P], wqkv[:, k, half * P:(half + 1) * P],
                                                gx[:, 0, k, :], start=(k == 0), stop=(k == KC - 1))
                last.then_inc(s_gqt_ps, 1)
                pe.wait_ge(s_gqt, t + 1)
                for h in range(HEADS):
                    n = t * HEADS + h
                    at = DK * (h % 4)
                    pe.wait_ge(s_gctx, n)
                    for c in range(BANKS):
                        last = nc.tensor.matmul(ps[:, c, :], gQT[at:at + DK, h // 4, :],
                                                gKT[at:at + DK, h // 4, c * BANK:(c + 1) * BANK], start=True, stop=True)
                    last.then_inc(s_gscores, 1)
                    pe.wait_ge(s_gprobs, n + 1)
                    for part in range(PT_PARTS):
                        if part:
                            pe.wait_ge(s_gpt, n * PT_PARTS + part)
                        for j in range(PT_TILES):
                            c = j * P
                            k = part * PT_TILES + j
                            last = nc.tensor.transpose(ps[:, c // BANK, c % BANK:c % BANK + P], gS[:, k * P:(k + 1) * P], ident[:])
                        last.then_inc(s_gpt_ps, 1)
                        pe.wait_ge(s_gpt, n * PT_PARTS + part + 1)
                        for j in range(PT_TILES):
                            k = part * PT_TILES + j
                            last = nc.tensor.matmul(ps[:, BANKS - 1, 0:DK], gPT[:, j * P:(j + 1) * P],
                                                    kv_all[:, k, D + h * DK:D + (h + 1) * DK], start=(k == 0), stop=(k == TILES - 1))
                    last.then_inc(s_gpv, 1)
                post_pe(pe, post, t, 0, s_gctx, (t + 1) * HEADS)

        @block.vector
        def _(dve):
            dve.wait_ge(s_const, CONSTS)
            with dve.Fori(0, TILES) as t:
                dve.wait_ge(s_gadj, (t + 1) * 16)
                nc.vector.tensor_tensor(gadj[:, bass.ds(t * P, P)], gadj[:, bass.ds(t * P, P)], ident[:], ALU.add).then_inc(s_gdiag, 1)
                dve.wait_ge(s_gdiag, t + 1)
                nc.vector.tensor_scalar(gmask[:], gadj[:], 0.0, NEG, ALU.is_equal, ALU.mult).then_inc(s_gmask, 1)
                dve.wait_ge(s_gmask, t + 1)
                for h in range(HEADS):
                    n = t * HEADS + h
                    dve.wait_ge(s_gscores, n + 1)
                    nc.vector.tensor_tensor(gS[:], flat(ps[:]), gmask[:], ALU.add).then_inc(s_gmasked, 1)
                    dve.wait_ge(s_gmasked, n + 1)
                    nc.vector.tensor_reduce(gstat[:, 0:1], gS[:], AX_X, ALU.max).then_inc(s_gmax, 1)
                    dve.wait_ge(s_gmax, n + 1)
                    nc.vector.tensor_scalar(gstat[:, 1:2], gstat[:, 0:1], -SCALE, None, ALU.mult).then_inc(s_gnm, 1)
                    dve.wait_ge(s_gprobs, n + 1)
                    nc.vector.reciprocal(gstat[:, 3:4], gstat[:, 2:3]).then_inc(s_grl, 1)
                    dve.wait_ge(s_grl, n + 1)
                    dve.wait_ge(s_gpv, n + 1)
                    nc.vector.tensor_scalar(post["ctx"][:, 0, h * DK:(h + 1) * DK], ps[:, BANKS - 1, 0:DK], gstat[:, 3:4], None,
                                            ALU.mult).then_inc(s_gctx, 1)
                dve.wait_ge(s_gctx, (t + 1) * HEADS)
                post_dve(dve, post, t, 0)


_DIRECT = ["x", "adj"]


def kernel(**inputs):
    import numpy as _np
    import concourse.bacc as _bacc
    from concourse import mybir as _mybir
    from concourse.bass_utils import run_bass_kernel_spmd as _run

    w = {k.replace("L0_gnn_", ""): _np.ascontiguousarray(v) for k, v in inputs.items()}
    arrays = {
        "x": w["x"],
        "xT": _np.ascontiguousarray(w["x"].T),
        "adj": w["adj"],
        "wqkvT": _np.ascontiguousarray(_np.concatenate([w["Wq"], w["Wk"], w["Wv"]]).T),
        "bq": _np.ascontiguousarray(w["bq"].reshape(-1, 128).T),
        "bk": _np.ascontiguousarray(w["bk"].reshape(-1, 128).T),
        "bqkv": _np.concatenate([w["bq"], w["bk"], w["bv"]]).reshape(1, -1),
        "woT": _np.ascontiguousarray(w["Wo"].T),
        "bo": w["bo"].reshape(1, -1),
        "w1T": _np.ascontiguousarray(w["W1"].T),
        "b1": _np.ascontiguousarray(w["b1"].reshape(-1, 128).T),
        "w2T": _np.ascontiguousarray(w["W2"].T),
        "b2": w["b2"].reshape(1, -1),
        "g1": w["ln1_g"].reshape(1, -1),
        "be1": w["ln1_b"].reshape(1, -1),
        "g2": w["ln2_g"].reshape(1, -1),
        "be2": w["ln2_b"].reshape(1, -1),
    }
    nc = _bacc.Bacc("TRN2", target_bir_lowering=False, num_devices=1)
    args = [nc.dram_tensor(f"in_{n}", a.shape, _mybir.dt.from_np(a.dtype), kind="ExternalInput").ap() for n, a in arrays.items()]
    args.append(nc.dram_tensor("out_dram", (4096, 256), _mybir.dt.float32, kind="ExternalOutput").ap())
    build(nc, *args)
    r = _run(nc, [{f"in_{n}": a for n, a in arrays.items()}], core_ids=[0])
    return r.results[0]["out_dram"]
```

```python
from contextlib import ExitStack

import concourse.bass as bass
from concourse import mybir

ALU = mybir.AluOpType
ACT = mybir.ActivationFunctionType
F32 = mybir.dt.float32
BF16 = mybir.dt.bfloat16
I32 = mybir.dt.int32
U32 = mybir.dt.uint32
AX_X = mybir.AxisListType.X

P = 128
N = 4096
D = 256
HEADS = 8
DK = D // HEADS
FF = 1024
EPS = 1e-5
TILES = N // P
GROUP = 4
GROUPS = TILES // GROUP
KC = D // P
FC = FF // P
SCALE = 1.0 / float(DK) ** 0.5
NEG = -1.0e9
MISSING = -1.0e30
BANK = 512
BANKS = 8
FOUND = 8

EDGES = [[0, 27, 94, 203, 353, 543, 774, 1047, 1360, 1713, 2108, 2544, 3020, 3537, N],
         [0, 448, 1792, N], [0, 448, 1792, N], [0, 1024, N]] + [[0, 1024, N]] * 4 + [[0, N]] * (TILES - 8)
ROOM = [16] + [8] * (TILES - 1)
CHUNKS = [1] + [2] * 7 + [3] * 8 + [3, 2, 2, 2] * 4
NSEG = [len(e) - 1 for e in EDGES]
NCH = [NSEG[t] * CHUNKS[t] for t in range(TILES)]
FILLS = [(c + 1) // 2 for c in NCH]
UNITS = sum(NSEG)
AHEAD = 16


def running(values):
    out = [0]
    for v in values:
        out.append(out[-1] + v)
    return out


U_AT = running(NSEG)
F_AT = running(FILLS)
G_AT = [sum(NCH[i] for i in range(t % 2, t, 2)) for t in range(TILES + 2)]


class At:

    def __init__(self, g, j, g0):
        self.g = g + j // GROUP if j >= GROUP else g
        self.j = j % GROUP
        self.g0 = g0 + j // GROUP
        self.rep = GROUP * self.g0 + self.j
        self.par = self.rep % 2
        if self.rep < TILES:
            self.nseg, self.room, self.per, self.nch = (NSEG[self.rep], ROOM[self.rep], CHUNKS[self.rep], NCH[self.rep])
            self.fills = FILLS[self.rep]

    @property
    def t(self):
        return self.g * GROUP + self.j

    def total(self, table):
        if isinstance(self.g, int):
            return table[GROUP * self.g + self.j]
        a = GROUP * self.g0 + self.j
        return table[a] + (self.g - self.g0) * (table[a + GROUP] - table[a])

    @property
    def first_fill(self):
        return sum(FILLS[GROUP * self.g0:self.rep])

    def next(self):
        return At(self.g, self.j + 1, self.g0)


def build(nc, x, xT, adj, wqkvT, bq, bk, bqkv, woT, bo, w1T, b1, w2T, b2, g1, be1, g2, be2, out):
    with ExitStack() as ctx:
        def sb(name, shape, dt=F32):
            return ctx.enter_context(nc.sbuf_tensor(name, shape, dt))

        def sem(name):
            return ctx.enter_context(nc.semaphore(name))

        def flat(ap):
            return ap.rearrange("p a b -> p (a b)")

        ps = ctx.enter_context(nc.psum_tensor("ps", [P, BANKS, BANK], F32))
        QE, SMALL, ELL, POST, ME, ACC = 0, 2, 3, 4, 6, 7

        wqkv = sb("wqkv", [P, KC, 3 * D])
        wo = sb("wo", [P, KC, D])
        w1 = sb("w1", [P, KC, FF])
        w2 = sb("w2", [P, FC, D])
        bias_qkv = sb("bias_qkv", [P, 3 * D])
        bias_qT = sb("bias_qT", [P, KC])
        bias_kT = sb("bias_kT", [P, KC])
        bias_1T = sb("bias_1T", [P, FC])
        rows = {n: sb("row_" + n, [P, D]) for n in ("bo", "b2", "g1", "be1", "g2", "be2")}

        ident = sb("ident", [P, P])
        not_ident = sb("not_ident", [P, P])
        before = sb("before", [P, P])
        all_ones = sb("all_ones", [P, P])
        neg_half = sb("neg_half", [P, GROUP])
        eps_col = sb("eps_col", [P, GROUP])
        row_1 = sb("row_1", [P, P])
        edge_no = sb("edge_no", [P, 3 * P])
        edge_col = sb("edge_col", [P, 3])
        slot_no = sb("slot_no", [P, max(ROOM)])
        ones8 = sb("ones8", [P, FOUND], I32)
        holds = sb("holds", [P, UNITS])

        q_all = sb("q_all", [P, TILES, D])
        kv_dram = nc.dram_tensor("kv_table", (N, 2 * D), F32, kind="Internal").ap()
        kv_self = [sb(f"kv_self{i}", [P, 2 * D]) for i in range(2)]

        WORDS = FOUND + 2
        adj_buf = [sb(f"adj_buf{i}", [P, N + FOUND], I32) for i in range(2)]
        counted_out = sb("counted_out", [P, N], mybir.dt.uint8)
        found = sb("found", [P, max(NSEG), max(ROOM)], U32)
        first_idx = sb("first_idx", [P, NSEG[0], ROOM[0] + 2])
        idx_all = sb("idx_all", [P, UNITS - NSEG[0], WORDS])
        counts = sb("counts", [P, UNITS])
        over = sb("over", [P, UNITS])
        neg_mid = sb("neg_mid", [P, UNITS])
        half = sb("half", [P, UNITS])
        bad = sb("bad", [P, 2, UNITS])

        MOST = [max(NCH[i::2]) for i in range(2)]
        REST = max(NCH[1:])
        rt = [sb(f"rt{i}", [P, REST, P]) for i in range(2)]
        onehot = [sb(f"onehot{i}", [P, REST, P]) for i in range(2)]
        spread = sb("spread", [P, REST * FOUND * HEADS])
        slot_hot = [sb(f"slot_hot{i}", [P, MOST[i] * (16 if i == 0 else 8)]) for i in range(2)]
        slot_of = [sb(f"slot_of{i}", [P, MOST[i]]) for i in range(2)]
        row_of = [sb(f"row_of{i}", [P, MOST[i]]) for i in range(2)]
        col_of = [sb(f"col_of{i}", [P, MOST[i]], U32) for i in range(2)]
        picked = sb("picked", [P, REST * FOUND])
        kv = [sb(f"kv{i}", [P, MOST[i], 2 * D]) for i in range(2)]
        product = [sb(f"product{i}", [P, 2, D]) for i in range(2)]
        product_self = sb("product_self", [P, D])
        s_e = sb("s_e", [P, MOST[0], HEADS])
        s_self = sb("s_self", [P, HEADS])
        absent = sb("absent", [P, max(NSEG[1:]) * FOUND])
        top = sb("top", [P, HEADS])
        top_all = sb("top_all", [P, HEADS])
        below = sb("below", [P, MOST[0] + 1, HEADS])
        spare_dve = sb("spare_dve", [P, GROUP])
        spare_pool = sb("spare_pool", [P, GROUP])
        recip = sb("recip", [P, HEADS])
        flag = sb("flag", [P, 1], I32)
        flag_f = sb("flag_f", [P, 1])

        s_const = sem("s_const")
        s_holds = sem("s_holds")
        HOLDS = len([t for t in range(TILES) if t == 0 or CHUNKS[t] != CHUNKS[t - 1]])
        s_weights = sem("s_weights")
        s_x = [sem("s_x0"), sem("s_x1")]
        s_qkv_ps = sem("s_qkv_ps")
        s_qkv_raw = sem("s_qkv_raw")
        s_qkv = sem("s_qkv")
        s_kv_out = [sem("s_kv_out0"), sem("s_kv_out1")]
        adj_loaded = [sem("adj_loaded0"), sem("adj_loaded1")]
        diag_clear = sem("diag_clear")
        counted = sem("counted")
        hunt = sem("hunt")
        extracted = sem("extracted")
        over_ready = sem("over_ready")
        starts_ps = sem("starts_ps")
        starts_link = sem("starts_link")
        starts_ready = sem("starts_ready")
        distance = sem("distance")
        rt_ready = sem("rt_ready")
        lists_ps = sem("lists_ps")
        slots_ready = sem("slots_ready")
        hot_ready = sem("hot_ready")
        picked_ready = sem("picked_ready")
        cols_ready = sem("cols_ready")
        onehot_ready = sem("onehot_ready")
        gathered = [sem("gathered0"), sem("gathered1")]
        self_loaded = [sem("self_loaded0"), sem("self_loaded1")]
        qe_ps = sem("qe_ps")
        product_ready = sem("product_ready")
        scores_ready = sem("scores_ready")
        self_product = sem("self_product")
        self_score = sem("self_score")
        spread_ready = sem("spread_ready")
        ell_ps = sem("ell_ps")
        absent_ready = sem("absent_ready")
        ell_masked = sem("ell_masked")
        top_ready = sem("top_ready")
        top_all_ready = sem("top_all_ready")
        me_ps = sem("me_ps")
        below_ready = sem("below_ready")
        probs_ready = sem("probs_ready")
        weighted = sem("weighted")
        acc_ps = sem("acc_ps")
        recip_ready = sem("recip_ready")
        ctx_ready = sem("ctx_ready")
        flag_link = sem("flag_link")
        flag_ready = sem("flag_ready")

        def post_signals(name):
            signals = ("x_loaded x_biased ctxT_ps ctxT_done attn_ps res1 mv1 rstd1 norm1 h1_done h1T_ps h1T "
                       "ff_ps ff h1_b2 out_ps res2 mv2 rstd2 norm2 final stored link plink").split()
            return {n: sem(name + n) for n in signals}

        post_shapes = {
            "ctx": [P, GROUP, D], "ctxT": [P, KC, GROUP * P], "x": [P, GROUP, D], "h1": [P, GROUP, D],
            "ffT": [P, FC, GROUP * P], "stats": [P, GROUP, 6], "mv": [P, GROUP, 2], "rstd": [P, GROUP], "spare": [P, 1],
        }
        x_h1 = sb("post_x_h1", [P, 2, GROUP, D])
        post_buffers = {n: sb("post_" + n, s) for n, s in post_shapes.items() if n not in ("x", "h1")}
        views = {**{n: b[:] for n, b in post_buffers.items()}, "x": x_h1[:, 0], "h1": x_h1[:, 1]}
        post = {"g": GROUP, **views, **post_signals("p_")}

        ff_flat = flat(post_buffers["ffT"][:])
        xbuf = ff_flat[:, 0:2 * KC * GROUP * P].rearrange("p (b k n) -> p b k n", b=2, k=KC)
        words = NCH[0] * ROOM[0] * HEADS
        spread_of = [ff_flat[:, 0:words], spread[:]]
        rt_of = [ff_flat[:, words:words + NCH[0] * P].rearrange("p (c n) -> p c n", n=P), rt[0][:], rt[1][:]]
        lots = words + NCH[0] * P
        picked_of = [ff_flat[:, lots:lots + NCH[0] * ROOM[0]], picked[:]]
        absent_of = [ff_flat[:, lots + NCH[0] * ROOM[0]:lots + 2 * NCH[0] * ROOM[0]], absent[:]]
        onehot_of = [x_h1[:].rearrange("p a b c -> p (a b c)")[:, 0:NCH[0] * P].rearrange("p (c n) -> p c n", n=P),
                     onehot[0][:], onehot[1][:]]

        gKT = q_all[:].rearrange("p t d -> p (t d)").rearrange("p (k n) -> p k n", k=KC)
        gmask = flat(kv[0][:])[:, 0:N]
        gS = adj_buf[1][:, 0:N].bitcast(F32)
        gadj = adj_buf[0][:, 0:N]
        gXT = xbuf[:, 0]
        gx = xbuf[:, 1, :, 0:P]
        g_small = flat(kv[1][:])
        gQT = g_small[:, 0:KC * P].rearrange("p (k n) -> p k n", k=KC)
        gPT = g_small[:, KC * P:KC * P + 8 * P]
        gV = g_small[:, KC * P + 8 * P:KC * P + 8 * P + TILES * DK].rearrange("p (t d) -> p t d", d=DK)
        gstat = sb("gstat", [P, 4])
        gpost = {"g": 1, **{n: (v[:, 0:1] if n in ("ctx", "x", "h1", "stats", "mv", "rstd") else v) for n, v in views.items()},
                 **post_signals("g_")}
        gpost["ctxT"] = post_buffers["ctxT"][:, :, 0:P]
        gpost["ffT"] = post_buffers["ffT"][:, :, 0:P]
        (s_gx, s_gkt_ps, s_gkt, s_gadj, s_gmask, s_gdiag, s_gxq, s_gqt_ps, s_gqt, s_gscores, s_gmasked, s_gmax, s_gnm,
         s_gprobs, s_gpt_ps, s_gpt, s_gpv, s_grl, s_gctx, s_gv) = [sem(n) for n in (
            "s_gx s_gkt_ps s_gkt s_gadj s_gmask s_gdiag s_gxq s_gqt_ps s_gqt s_gscores s_gmasked s_gmax s_gnm "
            "s_gprobs s_gpt_ps s_gpt s_gpv s_grl s_gctx s_gv").split()]

        WEIGHT_DMAS = 8 + len(rows)
        CONSTS = 18
        PT_TILES = 8
        PT_PARTS = TILES // PT_TILES
        x_rows = x.rearrange("(t p) d -> p t d", p=P)
        out_rows = out.rearrange("(t p) d -> p t d", p=P)
        xT_cols = xT.rearrange("(k p) n -> p k n", p=P)

        def wait(eng, s, value):
            if not isinstance(value, int) or value > 0:
                eng.wait_ge(s, value)



        def unit_range(q):
            return q.total(U_AT)

        def per_unit(table, q, u):
            at = unit_range(q) + u
            return table[:, bass.ds(at, 1)] if not isinstance(at, int) else table[:, at:at + 1]

        def lists(q, u):
            if q.rep == 0:
                return first_idx[:, u, :]
            at = unit_range(q) + u - NSEG[0]
            return flat(idx_all[:, bass.ds(at, 1), :]) if not isinstance(at, int) else idx_all[:, at, :]

        def buf(q):
            return 0 if q.rep == 0 else 1 + q.par

        def extract_dve(dve, q, n):
            a = adj_buf[q.par]
            cols = EDGES[q.rep]
            dve.wait_ge(adj_loaded[q.par], (q.g * 2 + q.j // 2 + 1) * 16)
            diag = a[:, bass.ds(q.t * P, P)] if not isinstance(q.t, int) else a[:, q.t * P:(q.t + 1) * P]
            wait(dve, extracted, q.t)
            nc.vector.tensor_tensor(diag, diag, not_ident[:], ALU.mult).then_inc(diag_clear, 1)
            dve.wait_ge(diag_clear, q.t + 1)
            if not isinstance(q.t, int):
                nc.vector.memset(spare_dve[:, q.j:q.j + 1], 0.0)
            for u in reversed(range(q.nseg)):
                lo, hi = cols[u], cols[u + 1]
                part = a[:, lo:hi + FOUND]
                if hi < N:
                    dve.wait_ge(counted, q.t + 1)
                    nc.vector.memset(a[:, hi:hi + FOUND], 1).then_inc(hunt, 1)
                    n = n + 1
                    dve.wait_ge(hunt, n)
                nc.vector.max_index(found[:, u, 0:FOUND], ones8[:], part).then_inc(hunt, 1)
                n = n + 1
                if q.room > FOUND:
                    dve.wait_ge(counted, q.t + 1)
                    dve.wait_ge(hunt, n)
                    nc.vector.match_replace(part, ones8[:], part, 0.0).then_inc(hunt, 1)
                    dve.wait_ge(hunt, n + 1)
                    nc.vector.memset(a[:, hi:hi + FOUND], 1).then_inc(hunt, 1)
                    dve.wait_ge(hunt, n + 2)
                    nc.vector.max_index(found[:, u, FOUND:2 * FOUND], ones8[:], part).then_inc(hunt, 1)
                    n = n + 3
                dve.wait_ge(hunt, n)
            for u in range(q.nseg):
                last = nc.vector.tensor_scalar(lists(q, u)[:, 0:q.room], found[:, u, 0:q.room], float(cols[u]), None, ALU.add)
            last.then_inc(extracted, 1)

        def hunts(t):
            return sum((1 if h < N else 0) + (4 if ROOM[t] > FOUND else 1) for h in EDGES[t][1:])

        HUNT_AT = running([hunts(t) for t in range(TILES)])

        def count_act(act, q):
            act.wait_ge(diag_clear, q.t + 1)
            wait(act, counted, q.t)
            for u in range(q.nseg):
                lo, hi = EDGES[q.rep][u], EDGES[q.rep][u + 1]
                last = nc.scalar.activation(counted_out[:, lo:hi], adj_buf[q.par][:, lo:hi], ACT.Copy,
                                            accum_out=per_unit(counts, q, u))
            last.then_inc(counted, 1)

        def units_of(table, g, g0):
            a, b = At(g, 0, g0), At(g, GROUP, g0)
            n = sum(NSEG[GROUP * g0:GROUP * g0 + GROUP])
            at = a.total(U_AT)
            return (table[:, bass.ds(at, n)] if not isinstance(at, int) else table[:, at:at + n]), n

        def starts_over(dve, g, g0):
            dve.wait_ge(counted, (g + 1) * GROUP)
            if g0 == 0:
                n0 = NSEG[0]
                nc.vector.tensor_scalar(over[:, 0:n0], counts[:, 0:n0], float(ROOM[0]), None, ALU.is_gt)
                n = U_AT[GROUP]
                nc.vector.tensor_scalar(over[:, n0:n], counts[:, n0:n], float(FOUND), None, ALU.is_gt).then_inc(over_ready, 1)
            else:
                c, n = units_of(counts, g, g0)
                nc.vector.tensor_scalar(units_of(over, g, g0)[0], c, float(FOUND), None, ALU.is_gt).then_inc(over_ready, 1)

        def starts_pe(pe, g, g0):
            c, n = units_of(counts, g, g0)
            pe.wait_ge(over_ready, g + 1)
            wait(pe, starts_ready, g)
            if isinstance(g, int):
                pe.wait_ge(counted, (g + 1) * GROUP)
            nc.tensor.matmul(ps[:, SMALL, 0:n], before[:], c, start=True, stop=True)
            nc.tensor.matmul(ps[:, SMALL, n:2 * n], all_ones[:], c, start=True, stop=True)
            nc.tensor.matmul(ps[:, SMALL, 2 * n:3 * n], all_ones[:], units_of(over, g, g0)[0], start=True, stop=True).then_inc(starts_ps, 1)

        def starts_dve(dve, g, g0):
            c, n = units_of(counts, g, g0)
            mid = units_of(neg_mid, g, g0)[0]
            small = ps[:, SMALL, :]
            nc.vector.tensor_scalar(mid, c, -0.5, 0.5, ALU.mult, ALU.add).then_inc(starts_link, 1)
            nc.vector.tensor_scalar(units_of(half, g, g0)[0], c, 0.5, -0.25, ALU.mult, ALU.add)
            dve.wait_ge(starts_ps, g + 1)
            dve.wait_ge(starts_link, g + 1)
            nc.vector.tensor_tensor(mid, mid, small[:, 0:n], ALU.subtract)
            at = At(g, 0, g0).total(U_AT)
            if g0 == 0:
                nc.vector.tensor_copy(first_idx[:, :, ROOM[0]], small[:, 0:NSEG[0]])
                nc.vector.tensor_copy(idx_all[:, 0:n - NSEG[0], FOUND], small[:, NSEG[0]:n])
                nc.vector.tensor_tensor(bad[:, 0, 0:n], small[:, n:2 * n], holds[:, 0:n], ALU.is_gt)
                nc.vector.tensor_copy(bad[:, 1, 0:n], small[:, 2 * n:3 * n]).then_inc(starts_ready, 1)
            else:
                there = bass.ds(at - NSEG[0], n) if not isinstance(at, int) else slice(at - NSEG[0], at - NSEG[0] + n)
                here = bass.ds(at, n) if not isinstance(at, int) else slice(at, at + n)
                nc.vector.tensor_copy(idx_all[:, there, FOUND], small[:, 0:n])
                nc.vector.tensor_tensor(bad[:, 0, here], small[:, n:2 * n], holds[:, here], ALU.is_gt)
                nc.vector.tensor_copy(bad[:, 1, here], small[:, 2 * n:3 * n]).then_inc(starts_ready, 1)

        def distance_act(act, q):
            wait(act, me_ps, q.t - 1)
            if q.rep == 0:
                act.wait_ge(s_qkv_ps, TILES)
            act.wait_ge(starts_ready, q.g + 1)
            for u in range(q.nseg):
                w = q.per * P
                last = nc.scalar.activation(flat(rt_of[buf(q)])[:, u * w:(u + 1) * w], edge_no[:, 0:w], ACT.Abs,
                                            bias=per_unit(neg_mid, q, u))
            last.then_inc(distance, 1)

        def rt_dve(dve, q):
            dve.wait_ge(distance, q.t + 1)
            for u in range(q.nseg):
                w = q.per * P
                part = flat(rt_of[buf(q)])[:, u * w:(u + 1) * w]
                last = nc.vector.tensor_scalar(part, part, per_unit(half, q, u), None, ALU.is_le)
            last.then_inc(rt_ready, 1)

        def lists_pe(pe, q, prefixes):
            pe.wait_ge(rt_ready, q.t + 1)
            pe.wait_ge(starts_ready, prefixes)
            wait(pe, onehot_ready, q.t)
            w = q.room + 2
            for c in range(q.nch):
                last = nc.tensor.matmul(ps[:, SMALL, c * w:(c + 1) * w], rt_of[buf(q)][:, c, :], lists(q, c // q.per),
                                        start=True, stop=True)
            last.then_inc(lists_ps, 1)

        def hot(q):
            return slot_hot[q.par][:, 0:q.nch * q.room].rearrange("p (c k) -> p c k", k=q.room)

        def cols_dve(dve, q):
            w = q.room + 2
            at = ps[:, SMALL, 0:q.nch * w].rearrange("p (c w) -> p c w", w=w)
            dve.wait_ge(lists_ps, q.t + 1)
            slots = slot_of[q.par][:, 0:q.nch]
            nc.vector.tensor_tensor(slots.rearrange("p (u c) -> p u c", c=q.per),
                                    edge_col[:, 0:q.per].unsqueeze(1).to_broadcast([P, q.nseg, q.per]),
                                    at[:, :, q.room].rearrange("p (u c) -> p u c", c=q.per), ALU.subtract).then_inc(slots_ready, 1)
            nc.vector.tensor_copy(row_of[q.par][:, 0:q.nch], at[:, :, q.room + 1])
            dve.wait_ge(slots_ready, q.t + 1)
            nc.vector.tensor_tensor(hot(q), slot_no[:, 0:q.room].unsqueeze(1).to_broadcast([P, q.nch, q.room]),
                                    slots.unsqueeze(2).to_broadcast([P, q.nch, q.room]), ALU.is_equal).then_inc(hot_ready, 1)
            dve.wait_ge(hot_ready, q.t + 1)
            wait(dve, cols_ready, q.t)
            pick = picked_of[1 if q.rep else 0][:, 0:q.nch * q.room].rearrange("p (c k) -> p c k", k=q.room)
            nc.vector.tensor_tensor(pick, hot(q), at[:, :, 0:q.room], ALU.mult).then_inc(picked_ready, 1)
            dve.wait_ge(picked_ready, q.t + 1)
            wait(dve, acc_ps, q.t - 1)
            with nc.allow_low_precision(reason="one whole number below 4096 and zeros"):
                nc.vector.tensor_reduce(col_of[q.par][:, 0:q.nch], pick, AX_X, ALU.add).then_inc(cols_ready, 1)
            for c in range(q.nch):
                last = nc.vector.tensor_scalar(onehot_of[buf(q)][:, c, :], row_1[:], row_of[q.par][:, c:c + 1], None, ALU.is_equal)
            last.then_inc(onehot_ready, 1)

        def gather_pool(pool, q):
            pool.wait_ge(cols_ready, q.t + 1)
            wait(pool, acc_ps, q.t - 1)
            if not isinstance(q.t, int):
                nc.gpsimd.tensor_tensor(spare_pool[:, q.j:q.j + 1], eps_col[:, 0:1], eps_col[:, 0:1], ALU.add)
            for c in range(q.nch):
                nc.gpsimd.indirect_dma_start(kv[q.par][:, c, :], None, kv_dram,
                                             bass.IndirectOffsetOnAxis(ap=col_of[q.par][:, c:c + 1], axis=0)
                                             ).then_inc(gathered[q.par], 16)

        def self_load(act, q):
            wait(act, acc_ps, q.t - 1)
            rows_at = bass.ds(q.t * P, P) if not isinstance(q.t, int) else slice(q.t * P, (q.t + 1) * P)
            act.dma_start(kv_self[q.par][:], kv_dram[rows_at, :]).then_inc(self_loaded[q.par], 16)

        def q_tile(q):
            return q_all[:, bass.ds(q.t, 1), :] if not isinstance(q.t, int) else q_all[:, q.t:q.t + 1, :]

        def fills(q):
            for f in range(q.fills):
                place = q.first_fill + f
                yield QE + place % 2, 2 * f, min(2, q.nch - 2 * f), place, q.total(F_AT) + f

        def spread_queries_pe(pe, q, only=None):
            for i, (bank, c0, n, place, number) in enumerate(fills(q)):
                wait(pe, product_ready, number if place == 0 else number - 1)
                for c in range(n):
                    last = nc.tensor.matmul(ps[:, bank, c * D:(c + 1) * D], rt_of[buf(q)][:, c0 + c, :], flat(q_tile(q)),
                                            start=True, stop=True)
                last.then_inc(qe_ps, 1)

        def scores_dve(dve, q):
            dve.wait_ge(gathered[q.par], (q.total(G_AT) + q.nch) * 16)
            for bank, c0, n, place, number in fills(q):
                dve.wait_ge(qe_ps, number + 1)
                wait(dve, scores_ready, number if place == 0 else number - 1)
                nc.vector.tensor_tensor(product[place % 2][:, 0:n, :], ps[:, bank, 0:n * D].rearrange("p (c d) -> p c d", d=D),
                                        kv[q.par][:, c0:c0 + n, 0:D], ALU.mult).then_inc(product_ready, 1)
                dve.wait_ge(product_ready, number + 1)
                if c0 == 0:
                    wait(dve, below_ready, q.t)
                nc.vector.tensor_reduce(s_e[:, c0:c0 + n, :].rearrange("p c h -> p (c h)"),
                                        product[place % 2][:, 0:n, :].rearrange("p c (h d) -> p (c h) d", d=DK), AX_X, ALU.add
                                        ).then_inc(scores_ready, 1)

        def self_dve(dve, q):
            dve.wait_ge(self_loaded[q.par], (q.g * 2 + q.j // 2 + 1) * 16)
            wait(dve, self_score, q.t)
            nc.vector.tensor_tensor(product_self[:].unsqueeze(1), q_tile(q), kv_self[q.par][:, 0:D].unsqueeze(1), ALU.mult).then_inc(self_product, 1)
            dve.wait_ge(self_product, q.t + 1)
            nc.vector.tensor_reduce(s_self[:], product_self[:].rearrange("p (h d) -> p h d", d=DK), AX_X, ALU.add).then_inc(self_score, 1)

        def spread_dve(dve, q):
            dve.wait_ge(scores_ready, q.total(F_AT) + q.fills)
            w = q.room * HEADS
            dst = spread_of[1 if q.rep else 0][:, 0:q.nch * w].rearrange("p (c k h) -> p c k h", k=q.room, h=HEADS)
            nc.vector.tensor_tensor(dst, hot(q).unsqueeze(3).to_broadcast([P, q.nch, q.room, HEADS]),
                                    s_e[:, 0:q.nch, :].unsqueeze(2).to_broadcast([P, q.nch, q.room, HEADS]), ALU.mult
                                    ).then_inc(spread_ready, 1)

        def ell_pe(pe, q):
            pe.wait_ge(spread_ready, q.t + 1)
            pe.wait_ge(onehot_ready, q.t + 1)
            w = q.room * HEADS
            for u in range(q.nseg):
                for c in range(q.per):
                    k = u * q.per + c
                    bank, off = ELL + u * w // BANK, u * w % BANK
                    last = nc.tensor.matmul(ps[:, bank, off:off + w], onehot_of[buf(q)][:, k, :],
                                            spread_of[1 if q.rep else 0][:, k * w:(k + 1) * w], start=(c == 0), stop=(c == q.per - 1))
            last.then_inc(ell_ps, 1)

        def top_dve(dve, q):
            wait(dve, ell_masked, q.t)
            for u in range(q.nseg):
                last = nc.vector.tensor_scalar(absent_of[1 if q.rep else 0][:, u * q.room:(u + 1) * q.room], slot_no[:, 0:q.room], per_unit(counts, q, u), MISSING,
                                               ALU.is_ge, ALU.mult)
            last.then_inc(absent_ready, 1)
            dve.wait_ge(absent_ready, q.t + 1)
            dve.wait_ge(ell_ps, q.t + 1)
            k = q.nseg * q.room
            masked = spread_of[1 if q.rep else 0][:, 0:k * HEADS]
            src = flat(ps[:, ELL:ELL + (k * HEADS + BANK - 1) // BANK, :])[:, 0:k * HEADS]
            nc.vector.tensor_tensor(masked.rearrange("p (k h) -> p k h", h=HEADS), src.rearrange("p (k h) -> p k h", h=HEADS),
                                    absent_of[1 if q.rep else 0][:, 0:k].unsqueeze(2).to_broadcast([P, k, HEADS]), ALU.add).then_inc(ell_masked, 1)
            dve.wait_ge(ell_masked, q.t + 1)
            nc.vector.tensor_reduce(top[:], masked.rearrange("p (k h) -> p h k", h=HEADS), AX_X, ALU.max).then_inc(top_ready, 1)
            dve.wait_ge(top_ready, q.t + 1)
            nc.vector.tensor_tensor(top_all[:], top[:], s_self[:], ALU.max).then_inc(top_all_ready, 1)

        def me_pe(pe, q):
            pe.wait_ge(top_all_ready, q.t + 1)
            for c in range(q.nch):
                last = nc.tensor.matmul(ps[:, ME, c * HEADS:(c + 1) * HEADS], rt_of[buf(q)][:, c, :], top_all[:], start=True, stop=True)
            last.then_inc(me_ps, 1)

        def below_dve(dve, q):
            dve.wait_ge(me_ps, q.t + 1)
            nc.vector.tensor_tensor(below[:, q.nch, :], s_self[:], top_all[:], ALU.subtract)
            nc.vector.tensor_tensor(flat(below[:, 0:q.nch, :]), flat(s_e[:, 0:q.nch, :]), ps[:, ME, 0:q.nch * HEADS], ALU.subtract
                                    ).then_inc(below_ready, 1)

        def probs_act(act, q):
            act.wait_ge(below_ready, q.t + 1)
            nc.scalar.activation(kv[q.par][:, 0:q.nch, D - HEADS:D], below[:, 0:q.nch, :], ACT.Exp, scale=SCALE)
            nc.scalar.activation(kv_self[q.par][:, D - HEADS:D], below[:, q.nch, :], ACT.Exp, scale=SCALE).then_inc(probs_ready, 1)

        def weight_dve(dve, q):
            dve.wait_ge(probs_ready, q.t + 1)
            for v, p, n in ((kv[q.par][:, 0:q.nch, D:2 * D], kv[q.par][:, 0:q.nch, D - HEADS:D], q.nch),
                            (kv_self[q.par][:, D:2 * D].unsqueeze(1), kv_self[q.par][:, D - HEADS:D].unsqueeze(1), 1)):
                v = v.rearrange("p c (h d) -> p c h d", d=DK)
                last = nc.vector.tensor_tensor(v, v, p.unsqueeze(3).to_broadcast([P, n, HEADS, DK]), ALU.mult)
            last.then_inc(weighted, 1)

        def sum_pe(pe, q):
            pe.wait_ge(weighted, q.t + 1)
            wait(pe, ctx_ready, q.t)
            w = slice(D - HEADS, 2 * D)
            for c in range(q.nch):
                nc.tensor.matmul(ps[:, ACC, 0:D + HEADS], onehot_of[buf(q)][:, c, :], kv[q.par][:, c, w], start=(c == 0), stop=False)
            nc.tensor.matmul(ps[:, ACC, 0:D + HEADS], ident[:], kv_self[q.par][:, w], start=False, stop=True).then_inc(acc_ps, 1)

        def ctx_dve(dve, q):
            dve.wait_ge(acc_ps, q.t + 1)
            wait(dve, ctx_ready, q.t)
            nc.vector.reciprocal(recip[:], ps[:, ACC, 0:HEADS]).then_inc(recip_ready, 1)
            dve.wait_ge(recip_ready, q.t + 1)
            if q.j == 0:
                wait(dve, post["ctxT_ps"], q.g)
            nc.vector.tensor_tensor(post["ctx"][:, q.j, :].rearrange("p (h d) -> p h d", d=DK),
                                    ps[:, ACC, HEADS:HEADS + D].rearrange("p (h d) -> p h d", d=DK),
                                    recip[:].unsqueeze(2).to_broadcast([P, HEADS, DK]), ALU.mult).then_inc(ctx_ready, 1)


        def post_load(sp, q, n, t):
            sp.dma_start(q["x"], x_rows[:, bass.ds(t, q["g"]), :] if not isinstance(t, int) else x_rows[:, t:t + q["g"], :]
                         ).then_inc(q["x_loaded"], 16)

        def post_store(sp, q, n, t):
            sp.wait_ge(q["final"], n + 1)
            sp.dma_start(out_rows[:, bass.ds(t, q["g"]), :] if not isinstance(t, int) else out_rows[:, t:t + q["g"], :], q["h1"]
                         ).then_inc(q["stored"], 16)

        def transposed(pe, src, g, bank, done):
            for k in range(KC):
                for j in range(g):
                    c = (k * g + j) * P
                    last = nc.tensor.transpose(ps[:, bank + c // BANK, c % BANK:c % BANK + P], src[:, j, k * P:(k + 1) * P], ident[:])
            last.then_inc(done, 1)

        def post_pe_ctx(pe, q, n, bank, ctx_sem, ctx_value):
            pe.wait_ge(ctx_sem, ctx_value)
            wait(pe, q["res2"], n)
            transposed(pe, q["ctx"], q["g"], bank, q["ctxT_ps"])

        def post_pe_attn(pe, q, n, bank):
            pe.wait_ge(q["ctxT_done"], n + 1)
            for j in range(q["g"]):
                for k in range(KC):
                    last = nc.tensor.matmul(ps[:, bank + j * D // BANK, j * D % BANK:j * D % BANK + D],
                                            q["ctxT"][:, k, j * P:(j + 1) * P], wo[:, k, :], start=(k == 0), stop=(k == KC - 1))
            last.then_inc(q["attn_ps"], 1)

        def post_pe_h1(pe, q, n, bank):
            pe.wait_ge(q["h1_done"], n + 1)
            transposed(pe, q["h1"], q["g"], bank, q["h1T_ps"])

        def post_pe_ff(pe, q, n, bank, fs):
            for f in fs:
                if f == 0:
                    pe.wait_ge(q["h1T"], n + 1)
                if f >= 2:
                    pe.wait_ge(q["ff"], n * FC + f - 1)
                for k in range(KC):
                    last = nc.tensor.matmul(ps[:, bank + f % 2, 0:q["g"] * P], w1[:, k, f * P:(f + 1) * P], q["ctxT"][:, k, :],
                                            start=(k == 0), stop=(k == KC - 1))
                last.then_inc(q["ff_ps"], 1)

        def post_pe_out(pe, q, n, bank, js):
            for j in js:
                if j == 0:
                    pe.wait_ge(q["ff"], (n + 1) * FC)
                for f in range(FC):
                    last = nc.tensor.matmul(ps[:, bank + j * D // BANK, j * D % BANK:j * D % BANK + D],
                                            q["ffT"][:, f, j * P:(j + 1) * P], w2[:, f, :], start=(f == 0), stop=(f == FC - 1))
                if j == q["g"] - 1:
                    last.then_inc(q["out_ps"], 1)

        def post_act_copy(act, q, n, bank, ready, done):
            w = KC * q["g"] * P
            act.wait_ge(q[ready], n + 1)
            src = flat(ps[:, bank:bank + (w + BANK - 1) // BANK, :])[:, 0:w]
            nc.scalar.copy(q["ctxT"], src.rearrange("p (k n) -> p k n", k=KC)).then_inc(q[done], 1)

        def post_act_ff(act, q, n, bank, fs):
            for f in fs:
                act.wait_ge(q["ff_ps"], n * FC + f + 1)
                nc.scalar.activation(q["ffT"][:, f, :], ps[:, bank + f % 2, 0:q["g"] * P], ACT.Relu,
                                     bias=bias_1T[:, f:f + 1]).then_inc(q["ff"], 1)

        def post_dve_sum(dve, q, n, bank, k):
            g = q["g"]
            w = g * D
            src = flat(ps[:, bank:bank + (w + BANK - 1) // BANK, :])[:, 0:w]
            ps_ready, other, add, res, mv_done = ((q["attn_ps"], q["x_biased"], q["x"], q["res1"], q["mv1"]) if k == 0 else
                                                  (q["out_ps"], q["h1_b2"], q["h1"], q["res2"], q["mv2"]))
            dve.wait_ge(ps_ready, n + 1)
            dve.wait_ge(other, n + 1)
            if k == 0:
                wait(dve, q["stored"], n * 16)
            nc.vector.tensor_tensor(flat(q["h1"]), src, flat(add), ALU.add).then_inc(res, 1)
            dve.wait_ge(res, n + 1)
            for j in range(g):
                last = nc.vector.bn_stats(q["stats"][:, j, :], q["h1"][:, j, :])
            last.then_inc(q["link"], 1)
            dve.wait_ge(q["link"], n * 2 + 1 + k)
            nc.vector.memset(q["spare"], 0.0)
            for j in range(g):
                last = nc.vector.bn_aggr(q["mv"][:, j, :], q["stats"][:, j, :])
            last.then_inc(mv_done, 1)

        def post_dve_norm(dve, q, n, k):
            dve.wait_ge(q["rstd2" if k else "rstd1"], n + 1)
            for j in range(q["g"]):
                last = nc.vector.tensor_scalar(q["h1"][:, j, :], q["h1"][:, j, :], q["mv"][:, j, 0:1], q["rstd"][:, j:j + 1],
                                               ALU.subtract, ALU.mult)
            last.then_inc(q["norm2" if k else "norm1"], 1)

        def wide(name, g):
            return rows[name][:].unsqueeze(1).to_broadcast([P, g, D])

        def post_pool_bias(pool, q, n):
            pool.wait_ge(q["x_loaded"], (n + 1) * 16)
            nc.gpsimd.tensor_tensor(q["x"], q["x"], wide("bo", q["g"]), ALU.add).then_inc(q["x_biased"], 1)

        def post_pool_rstd(pool, q, n, k):
            g = q["g"]
            pool.wait_ge(q["mv2" if k else "mv1"], n + 1)
            nc.gpsimd.tensor_tensor(q["rstd"], q["mv"][:, :, 1], eps_col[:, 0:g], ALU.add).then_inc(q["plink"], 1)
            pool.wait_ge(q["plink"], n * 4 + 2 * k + 1)
            nc.gpsimd.tensor_tensor(q["rstd"], q["rstd"], neg_half[:, 0:g], ALU.pow).then_inc(q["rstd2" if k else "rstd1"], 1)

        def post_pool_affine(pool, q, n, k):
            g = q["g"]
            pool.wait_ge(q["norm2" if k else "norm1"], n + 1)
            nc.gpsimd.tensor_tensor(q["h1"], q["h1"], wide("g2" if k else "g1", g), ALU.mult).then_inc(q["plink"], 1)
            pool.wait_ge(q["plink"], n * 4 + 2 * k + 2)
            nc.gpsimd.tensor_tensor(q["h1"], q["h1"], wide("be2" if k else "be1", g), ALU.add).then_inc(q["final" if k else "h1_done"], 1)

        def post_pool_b2(pool, q, n):
            pool.wait_ge(q["h1T_ps"], n + 1)
            nc.gpsimd.tensor_tensor(q["h1"], q["h1"], wide("b2", q["g"]), ALU.add).then_inc(q["h1_b2"], 1)


        def general_sync(sp):
            with sp.Fori(0, GROUPS) as c:
                sp.wait_ge(s_gkt, c * KC)
                sp.dma_start(gXT, xT_cols[:, :, bass.ds(c * GROUP * P, GROUP * P)]).then_inc(s_gx, 16)
            with sp.Fori(0, TILES) as t:
                sp.wait_ge(s_gqt_ps, t)
                sp.dma_start(gx, xT_cols[:, :, bass.ds(t * P, P)]).then_inc(s_gxq, 16)
                sp.wait_ge(s_gmask, t)
                sp.dma_start(gadj, adj[bass.ds(t * P, P), :]).then_inc(s_gadj, 16)
                for h in range(HEADS):
                    sp.wait_ge(s_gpv, t * HEADS + h)
                    sp.dma_start(gV, kv_dram.rearrange("(t p) d -> p t d", p=P)[:, :, D + h * DK:D + (h + 1) * DK]).then_inc(s_gv, 16)
                post_load(sp, gpost, t, t)
                post_store(sp, gpost, t, t)
            sp.wait_ge(gpost["stored"], TILES * 16)

        def general_pool(pool):
            with pool.Fori(0, TILES) as t:
                post_pool_bias(pool, gpost, t)
                post_pool_rstd(pool, gpost, t, 0)
                post_pool_affine(pool, gpost, t, 0)
                post_pool_b2(pool, gpost, t)
                post_pool_rstd(pool, gpost, t, 1)
                post_pool_affine(pool, gpost, t, 1)

        def general_act(act):
            with act.Fori(0, GROUPS) as c:
                for part in range(KC):
                    act.wait_ge(s_gkt_ps, c * KC + part + 1)
                    nc.scalar.activation(gKT[:, part, bass.ds(c * GROUP * P, GROUP * P)], ps[:, part, :], ACT.Identity,
                                         bias=bias_kT[:, part:part + 1]).then_inc(s_gkt, 1)
            with act.Fori(0, TILES) as t:
                act.wait_ge(s_gqt_ps, t + 1)
                for part in range(KC):
                    last = nc.scalar.activation(gQT[:, part, :], ps[:, 0, part * P:(part + 1) * P], ACT.Identity,
                                                bias=bias_qT[:, part:part + 1])
                last.then_inc(s_gqt, 1)
                for h in range(HEADS):
                    n = t * HEADS + h
                    act.wait_ge(s_gnm, n + 1)
                    nc.scalar.activation(gS, gS, ACT.Exp, bias=gstat[:, 1:2], scale=SCALE,
                                         accum_out=gstat[:, 2:3]).then_inc(s_gprobs, 1)
                    for part in range(PT_PARTS):
                        act.wait_ge(s_gpt_ps, n * PT_PARTS + part + 1)
                        nc.scalar.copy(gPT, flat(ps[:, 0:PT_TILES * P // BANK, :])).then_inc(s_gpt, 1)
                post_act_copy(act, gpost, t, 0, "ctxT_ps", "ctxT_done")
                post_act_copy(act, gpost, t, 0, "h1T_ps", "h1T")
                post_act_ff(act, gpost, t, 0, range(FC))

        def general_pe(pe):
            with pe.Fori(0, GROUPS) as c:
                pe.wait_ge(s_gx, (c + 1) * 16)
                pe.wait_ge(s_gkt, c * KC)
                for part in range(KC):
                    for k in range(KC):
                        last = nc.tensor.matmul(ps[:, part, :], wqkv[:, k, D + part * P:D + (part + 1) * P], gXT[:, k, :],
                                                start=(k == 0), stop=(k == KC - 1))
                    last.then_inc(s_gkt_ps, 1)
            pe.wait_ge(s_gkt, GROUPS * KC)
            with pe.Fori(0, TILES) as t:
                pe.wait_ge(gpost["res2"], t)
                pe.wait_ge(s_gxq, (t + 1) * 16)
                for part in range(KC):
                    for k in range(KC):
                        last = nc.tensor.matmul(ps[:, 0, part * P:(part + 1) * P], wqkv[:, k, part * P:(part + 1) * P],
                                                gx[:, k, :], start=(k == 0), stop=(k == KC - 1))
                last.then_inc(s_gqt_ps, 1)
                pe.wait_ge(s_gqt, t + 1)
                for h in range(HEADS):
                    n = t * HEADS + h
                    at = DK * (h % 4)
                    pe.wait_ge(s_gctx, n)
                    for c in range(BANKS):
                        last = nc.tensor.matmul(ps[:, c, :], gQT[at:at + DK, h // 4, :],
                                                gKT[at:at + DK, h // 4, c * BANK:(c + 1) * BANK], start=True, stop=True)
                    last.then_inc(s_gscores, 1)
                    pe.wait_ge(s_gv, (n + 1) * 16)
                    pe.wait_ge(s_gprobs, n + 1)
                    for part in range(PT_PARTS):
                        for j in range(PT_TILES):
                            c = j * P
                            k = part * PT_TILES + j
                            last = nc.tensor.transpose(ps[:, c // BANK, c % BANK:c % BANK + P], gS[:, k * P:(k + 1) * P], ident[:])
                        last.then_inc(s_gpt_ps, 1)
                        pe.wait_ge(s_gpt, n * PT_PARTS + part + 1)
                        for j in range(PT_TILES):
                            k = part * PT_TILES + j
                            last = nc.tensor.matmul(ps[:, BANKS - 1, 0:DK], gPT[:, j * P:(j + 1) * P], gV[:, k, :],
                                                    start=(k == 0), stop=(k == TILES - 1))
                    last.then_inc(s_gpv, 1)
                post_pe_ctx(pe, gpost, t, 0, s_gctx, (t + 1) * HEADS)
                post_pe_attn(pe, gpost, t, 0)
                post_pe_h1(pe, gpost, t, 0)
                post_pe_ff(pe, gpost, t, 0, range(FC))
                post_pe_out(pe, gpost, t, 0, range(1))

        def general_dve(dve):
            with dve.Fori(0, TILES) as t:
                dve.wait_ge(s_gadj, (t + 1) * 16)
                nc.vector.tensor_tensor(gadj[:, bass.ds(t * P, P)], gadj[:, bass.ds(t * P, P)], ident[:], ALU.add).then_inc(s_gdiag, 1)
                dve.wait_ge(s_gdiag, t + 1)
                nc.vector.tensor_scalar(gmask, gadj, 0.0, NEG, ALU.is_equal, ALU.mult).then_inc(s_gmask, 1)
                dve.wait_ge(s_gmask, t + 1)
                for h in range(HEADS):
                    n = t * HEADS + h
                    dve.wait_ge(s_gscores, n + 1)
                    nc.vector.tensor_tensor(gS, flat(ps[:]), gmask, ALU.add).then_inc(s_gmasked, 1)
                    dve.wait_ge(s_gmasked, n + 1)
                    nc.vector.tensor_reduce(gstat[:, 0:1], gS, AX_X, ALU.max).then_inc(s_gmax, 1)
                    dve.wait_ge(s_gmax, n + 1)
                    nc.vector.tensor_scalar(gstat[:, 1:2], gstat[:, 0:1], -SCALE, None, ALU.mult).then_inc(s_gnm, 1)
                    dve.wait_ge(s_gprobs, n + 1)
                    nc.vector.reciprocal(gstat[:, 3:4], gstat[:, 2:3]).then_inc(s_grl, 1)
                    dve.wait_ge(s_grl, n + 1)
                    dve.wait_ge(s_gpv, n + 1)
                    nc.vector.tensor_scalar(gpost["ctx"][:, 0, h * DK:(h + 1) * DK], ps[:, BANKS - 1, 0:DK], gstat[:, 3:4], None,
                                            ALU.mult).then_inc(s_gctx, 1)
                post_dve_sum(dve, gpost, t, 0, 0)
                post_dve_norm(dve, gpost, t, 0)
                post_dve_sum(dve, gpost, t, 0, 1)
                post_dve_norm(dve, gpost, t, 1)

        def general(eng, path):
            eng.wait_ge(flag_ready, 1)
            eng.wait_ge(post["stored"], GROUPS * 16)
            raised = eng.value_load(flag[0:1, 0:1], min_val=0, max_val=1)
            with eng.If(raised > 0):
                path(eng)
            eng.wait_ge(flag_ready, 1)


        def loops(eng, group):
            group(0, 0)
            group(1, 1)
            with eng.Fori(2, 4) as g:
                group(g, 2)
            with eng.Fori(4, GROUPS - 1) as g:
                group(g, 4)
            group(GROUPS - 1, GROUPS - 1)

        block = ctx.enter_context(nc.Block())

        @block.sync
        def _(sp):
            def load_adj(q):
                wait(sp, extracted, q.t - 1)
                wait(sp, counted, q.t - 1)
                rows_at = bass.ds(q.t * P, P) if not isinstance(q.t, int) else slice(q.t * P, (q.t + 1) * P)
                sp.dma_start(adj_buf[q.par][:, 0:N], adj[rows_at, :]).then_inc(adj_loaded[q.par], 16)

            def load_x(c):
                wait(sp, s_qkv_ps, (c - 1) * GROUP)
                sp.dma_start(xbuf[:, c % 2], xT_cols[:, :, c * GROUP * P:(c + 1) * GROUP * P]).then_inc(s_x[c % 2], 16)

            load_x(0)
            load_x(1)
            load_adj(At(0, 0, 0))
            load_adj(At(0, 1, 0))
            for k in range(1, AHEAD // 2):
                for t in (2 * k, 2 * k + 1):
                    load_adj(At(t // GROUP, t % GROUP, t // GROUP))
                if k + 1 < GROUPS:
                    load_x(k + 1)
            with sp.Fori(AHEAD // GROUP, GROUPS) as g:
                for j in range(GROUP):
                    load_adj(At(g, j, AHEAD // GROUP))
            general(sp, general_sync)

        @block.gpsimd
        def _(pool):
            for t, v in ((ident, 0.0), (neg_half, -0.5), (eps_col, EPS), (not_ident, 1.0), (before, 1.0), (all_ones, 1.0),
                         (ones8, 1)):
                nc.gpsimd.memset(t[:], v).then_inc(s_const, 1)
            for b in adj_buf:
                nc.gpsimd.memset(b[:, N:N + FOUND], 1).then_inc(s_const, 1)
            pool.wait_ge(s_const, 9)
            diagonal = [[-1, P]]
            nc.gpsimd.affine_select(out=ident[:], in_=ident[:], compare_op=ALU.not_equal, fill=1.0, base=0,
                                    pattern=diagonal, channel_multiplier=1).then_inc(s_const, 1)
            nc.gpsimd.affine_select(out=not_ident[:], in_=not_ident[:], compare_op=ALU.not_equal, fill=0.0, base=0,
                                    pattern=diagonal, channel_multiplier=1).then_inc(s_const, 1)
            nc.gpsimd.affine_select(out=before[:], in_=before[:], compare_op=ALU.is_gt, fill=0.0, base=0,
                                    pattern=[[1, P]], channel_multiplier=-1).then_inc(s_const, 1)
            exact = {"allow_small_or_imprecise_dtypes": True}
            nc.gpsimd.iota(row_1[:], [[1, P]], base=1, channel_multiplier=0, **exact).then_inc(s_const, 1)
            nc.gpsimd.iota(edge_no[:], [[1, 3 * P]], base=0, channel_multiplier=0, **exact).then_inc(s_const, 1)
            nc.gpsimd.iota(edge_col[:], [[P, 3]], base=0, channel_multiplier=1, **exact).then_inc(s_const, 1)
            nc.gpsimd.iota(slot_no[:], [[1, max(ROOM)]], base=0, channel_multiplier=0, **exact).then_inc(s_const, 1)
            nc.gpsimd.iota(first_idx[:, :, ROOM[0] + 1], [[0, NSEG[0]]], base=1, channel_multiplier=1, **exact).then_inc(s_const, 1)
            nc.gpsimd.iota(idx_all[:, :, FOUND + 1], [[0, UNITS - NSEG[0]]], base=1, channel_multiplier=1, **exact).then_inc(s_const, 1)
            u = 0
            while u < UNITS:
                t = [i for i in range(TILES) if U_AT[i] <= u < U_AT[i + 1]][0]
                end = t
                while end < TILES and CHUNKS[end] == CHUNKS[t]:
                    end += 1
                nc.gpsimd.memset(holds[:, u:U_AT[end]], float(CHUNKS[t] * P)).then_inc(s_holds, 1)
                u = U_AT[end]
            pool.wait_ge(s_weights, 16 * WEIGHT_DMAS)
            with pool.Fori(0, TILES // 2) as i:
                for par in range(2):
                    t = i * 2 + par
                    pool.wait_ge(s_qkv_raw, t + 1)
                    nc.gpsimd.tensor_tensor(q_all[:, bass.ds(t, 1), :], q_all[:, bass.ds(t, 1), :],
                                            bias_qkv[:, 0:D].unsqueeze(1), ALU.add)
                    nc.gpsimd.tensor_tensor(kv_self[par][:], kv_self[par][:], bias_qkv[:, D:3 * D], ALU.add).then_inc(s_qkv, 1)
                    pool.wait_ge(s_qkv, t + 1)
                    pool.dma_start(kv_dram[bass.ds(t * P, P), :], kv_self[par][:]).then_inc(s_kv_out[par], 16)
            for par in range(2):
                pool.wait_ge(s_kv_out[par], TILES // 2 * 16)
            gather_pool(pool, At(0, 0, 0))

            def group(g, g0):
                n = g - 1
                for j in range(GROUP):
                    q = At(g, j, g0)
                    if j == 0 and g0 > 1:
                        post_pool_rstd(pool, post, n - 1, 1)
                    if j == 1 and g0 > 0:
                        post_pool_rstd(pool, post, n, 0)
                    if q.rep + 1 < TILES:
                        gather_pool(pool, q.next())
                    if j == 0 and g0 > 1:
                        post_pool_affine(pool, post, n - 1, 1)
                        post_store(pool, post, n - 1, (n - 1) * GROUP)
                    if j == 0 and g0 > 0:
                        post_pool_bias(pool, post, n)
                    if j == 1 and g0 > 0:
                        post_pool_affine(pool, post, n, 0)
                    if j == 2 and g0 > 0:
                        post_pool_b2(pool, post, n)

            loops(pool, group)
            for n in (GROUPS - 2, GROUPS - 1):
                if n == GROUPS - 1:
                    post_pool_bias(pool, post, n)
                    post_pool_rstd(pool, post, n, 0)
                    post_pool_affine(pool, post, n, 0)
                    post_pool_b2(pool, post, n)
                post_pool_rstd(pool, post, n, 1)
                post_pool_affine(pool, post, n, 1)
                post_store(pool, post, n, n * GROUP)
            general(pool, general_pool)

        @block.scalar
        def _(act):
            for dst, src in ((wqkv, wqkvT.rearrange("(k p) n -> p k n", p=P)), (bias_qkv, bqkv.to_broadcast([P, 3 * D])),
                             (wo, woT.rearrange("(k p) n -> p k n", p=P)),
                             (w1, w1T.rearrange("(k p) n -> p k n", p=P)), (w2, w2T.rearrange("(k p) n -> p k n", p=P)),
                             (bias_qT, bq), (bias_kT, bk), (bias_1T, b1)):
                act.dma_start(dst[:], src).then_inc(s_weights, 16)
            for name, src in (("bo", bo), ("b2", b2), ("g1", g1), ("be1", be1), ("g2", g2), ("be2", be2)):
                act.dma_start(rows[name][:], src.to_broadcast([P, D])).then_inc(s_weights, 16)

            def take(t, par, i):
                act.wait_ge(s_qkv_ps, t + 1)
                wait(act, s_kv_out[par], i * 16)
                nc.scalar.copy(kv_self[par][:], ps[:, 6 * par, :])
                q_at = q_all[:, bass.ds(t, 1), :] if not isinstance(t, int) else q_all[:, t:t + 1, :]
                nc.scalar.copy(q_at, ps[:, 6 * par + 1:6 * par + 2, 0:D]).then_inc(s_qkv_raw, 1)

            for i in range(8):
                take(2 * i, 0, i)
                take(2 * i + 1, 1, i)
                count_act(act, At(i // GROUP, i % GROUP, i // GROUP))
            with act.Fori(2, 4) as g:
                for j in range(GROUP):
                    for par in range(2):
                        take(g * 8 + 2 * j + par, par, g * GROUP + j)
                    count_act(act, At(g, j, 2))
            for par in range(2):
                act.wait_ge(s_kv_out[par], TILES // 2 * 16)
            self_load(act, At(0, 0, 0))
            distance_act(act, At(0, 0, 0))
            distance_act(act, At(0, 1, 0))

            def group(g, g0):
                n = g - 1
                for j in range(GROUP):
                    q = At(g, j, g0)
                    later = g0 > 0
                    if q.rep + 1 < TILES:
                        self_load(act, q.next())
                    if j == 0 and later:
                        post_act_copy(act, post, n, POST, "ctxT_ps", "ctxT_done")
                    if j == 2 and later:
                        post_act_copy(act, post, n, POST, "h1T_ps", "h1T")
                        post_act_ff(act, post, n, POST, range(0, 4))
                    if j == 3 and later:
                        post_act_ff(act, post, n, POST, range(6, 8))
                    probs_act(act, q)
                    if j == 2 and later:
                        post_act_ff(act, post, n, POST, range(4, 6))
                    if q.rep + 2 < TILES:
                        distance_act(act, q.next().next())
                    if g0 < 4:
                        count_act(act, At(g, j + AHEAD, g0))
                    if j == 3:
                        wait(act, post["res1"], g)
                        act.wait_ge(acc_ps, 1)
                        post_load(act, post, g, g * GROUP)

            loops(act, group)
            n = GROUPS - 1
            post_act_copy(act, post, n, POST, "ctxT_ps", "ctxT_done")
            post_act_copy(act, post, n, POST, "h1T_ps", "h1T")
            post_act_ff(act, post, n, POST, range(FC))
            general(act, general_act)

        @block.tensor
        def _(pe):
            pe.wait_ge(s_weights, 16 * WEIGHT_DMAS)
            pe.wait_ge(s_const, CONSTS)

            def project(i):
                for half_no in range(2):
                    pe.wait_ge(s_x[half_no], (i + 1) * 16)
                    for r in range(GROUP):
                        bank = 6 * (r % 2)
                        wait(pe, s_qkv_raw, (i * 2 + half_no) * GROUP + r - 1)
                        for at, cols in ((bank, slice(D, 3 * D)), (bank + 1, slice(0, D))):
                            for k in range(KC):
                                last = nc.tensor.matmul(ps[:, at, 0:cols.stop - cols.start], xbuf[:, half_no, k, r * P:(r + 1) * P],
                                                        wqkv[:, k, cols], start=(k == 0), stop=(k == KC - 1))
                        last.then_inc(s_qkv_ps, 1)

            project(0)
            with pe.Fori(1, GROUPS // 2) as i:
                project(i)
            pe.wait_ge(s_qkv, TILES)
            for g in range(4):
                starts_pe(pe, g, g)
            lists_pe(pe, At(0, 0, 0), 4)
            spread_queries_pe(pe, At(0, 0, 0))

            def group(g, g0):
                n = g - 1
                for j in range(GROUP):
                    q = At(g, j, g0)
                    later = g0 > 0
                    if q.rep + 1 < TILES:
                        lists_pe(pe, q.next(), g + 4 if g0 < 4 else GROUPS)
                    if later and j == 0:
                        post_pe_ctx(pe, post, n, POST, ctx_ready, g * GROUP)
                    if later and j == 2:
                        post_pe_ff(pe, post, n, POST, range(0, 2))
                    if later and j == 3:
                        post_pe_ff(pe, post, n, POST, range(6, 8))
                    ell_pe(pe, q)
                    if later and j == 2:
                        post_pe_ff(pe, post, n, POST, range(2, 4))
                    if later and j == 3:
                        post_pe_out(pe, post, n, POST, range(0, 1))
                    me_pe(pe, q)
                    if later and j == 0:
                        post_pe_attn(pe, post, n, POST)
                    if later and j == 2:
                        post_pe_ff(pe, post, n, POST, range(4, 5))
                    if later and j == 3:
                        post_pe_out(pe, post, n, POST, range(1, 2))
                    sum_pe(pe, q)
                    if later and j == 1:
                        post_pe_h1(pe, post, n, POST)
                    if later and j == 2:
                        post_pe_ff(pe, post, n, POST, range(5, 6))
                    if later and j == 3:
                        post_pe_out(pe, post, n, POST, range(2, 4))
                    if q.rep + 1 < TILES:
                        spread_queries_pe(pe, q.next())
                if g0 < 4:
                    starts_pe(pe, g + 4, g0 + 4)

            loops(pe, group)
            n = GROUPS - 1
            post_pe_ctx(pe, post, n, POST, ctx_ready, TILES)
            post_pe_attn(pe, post, n, POST)
            post_pe_h1(pe, post, n, POST)
            post_pe_ff(pe, post, n, POST, range(FC))
            post_pe_out(pe, post, n, POST, range(GROUP))
            general(pe, general_pe)

        @block.vector
        def _(dve):
            dve.wait_ge(s_const, CONSTS)
            dve.wait_ge(s_holds, HOLDS)

            def extract(g, j, g0):
                q = At(g, j, g0)
                extract_dve(dve, q, q.total(HUNT_AT))

            for g in range(2):
                for j in range(GROUP):
                    extract(g, j, g)
                starts_over(dve, g, g)
            with dve.Fori(2, 4) as g:
                for j in range(GROUP):
                    extract(g, j, 2)
                starts_over(dve, g, 2)
            for g in range(4):
                starts_dve(dve, g, g)
            rt_dve(dve, At(0, 0, 0))
            cols_dve(dve, At(0, 0, 0))

            def group(g, g0):
                n = g - 1
                for j in range(GROUP):
                    q = At(g, j, g0)
                    later = g0 > 0
                    if g0 > 1 and j == 0:
                        post_dve_sum(dve, post, n - 1, POST, 1)
                    if later and j == 1:
                        post_dve_sum(dve, post, n, POST, 0)
                    if q.rep + 1 < TILES:
                        rt_dve(dve, q.next())
                    scores_dve(dve, q)
                    self_dve(dve, q)
                    spread_dve(dve, q)
                    if g0 > 1 and j == 0:
                        post_dve_norm(dve, post, n - 1, 1)
                    if later and j == 1:
                        post_dve_norm(dve, post, n, 0)
                    if q.rep + 1 < TILES:
                        cols_dve(dve, q.next())
                    top_dve(dve, q)
                    if g0 < 4:
                        extract(g, j + AHEAD, g0)
                    below_dve(dve, q)
                    weight_dve(dve, q)
                    ctx_dve(dve, q)
                if g0 < 4:
                    starts_over(dve, g + 4, g0 + 4)
                    starts_dve(dve, g + 4, g0 + 4)

            loops(dve, group)
            for n in (GROUPS - 2, GROUPS - 1):
                for k in ((1,) if n == GROUPS - 2 else (0, 1)):
                    post_dve_sum(dve, post, n, POST, k)
                    post_dve_norm(dve, post, n, k)
            nc.vector.tensor_reduce(flag_f[:], flat(bad[:]), AX_X, ALU.max).then_inc(flag_link, 1)
            dve.wait_ge(flag_link, 1)
            nc.vector.tensor_scalar(flag[:], flag_f[:], 0.0, None, ALU.is_gt).then_inc(flag_ready, 1)
            general(dve, general_dve)


def kernel(**inputs):
    import numpy as _np
    import concourse.bacc as _bacc
    from concourse import mybir as _mybir
    from concourse.bass_utils import run_bass_kernel_spmd as _run

    w = {k.replace("L0_gnn_", ""): _np.ascontiguousarray(v) for k, v in inputs.items()}
    arrays = {
        "x": w["x"],
        "xT": _np.ascontiguousarray(w["x"].T),
        "adj": w["adj"],
        "wqkvT": _np.ascontiguousarray(_np.concatenate([w["Wq"], w["Wk"], w["Wv"]]).T),
        "bq": _np.ascontiguousarray(w["bq"].reshape(-1, 128).T),
        "bk": _np.ascontiguousarray(w["bk"].reshape(-1, 128).T),
        "bqkv": _np.concatenate([w["bq"], w["bk"], w["bv"]]).reshape(1, -1),
        "woT": _np.ascontiguousarray(w["Wo"].T),
        "bo": w["bo"].reshape(1, -1),
        "w1T": _np.ascontiguousarray(w["W1"].T),
        "b1": _np.ascontiguousarray(w["b1"].reshape(-1, 128).T),
        "w2T": _np.ascontiguousarray(w["W2"].T),
        "b2": w["b2"].reshape(1, -1),
        "g1": w["ln1_g"].reshape(1, -1),
        "be1": w["ln1_b"].reshape(1, -1),
        "g2": w["ln2_g"].reshape(1, -1),
        "be2": w["ln2_b"].reshape(1, -1),
    }
    nc = _bacc.Bacc("TRN2", target_bir_lowering=False, num_devices=1)
    args = [nc.dram_tensor(f"in_{n}", a.shape, _mybir.dt.from_np(a.dtype), kind="ExternalInput").ap() for n, a in arrays.items()]
    args.append(nc.dram_tensor("out_dram", (4096, 256), _mybir.dt.float32, kind="ExternalOutput").ap())
    build(nc, *args)
    r = _run(nc, [{f"in_{n}": a for n, a in arrays.items()}], core_ids=[0])
    return r.results[0]["out_dram"]
```

```python
from contextlib import ExitStack

import concourse.bass as bass
from concourse import mybir

ALU = mybir.AluOpType
ACT = mybir.ActivationFunctionType
F32 = mybir.dt.float32
I32 = mybir.dt.int32
U32 = mybir.dt.uint32
AX_X = mybir.AxisListType.X

P = 128
N = 4096
D = 256
HEADS = 8
DK = D // HEADS
FF = 1024
EPS = 1e-5
TILES = N // P
GROUP = 4
GROUPS = TILES // GROUP
KC = D // P
FC = FF // P
SCALE = 1.0 / float(DK) ** 0.5
NEG = -1.0e9
MISSING = -1.0e30
BANK = 512
BANKS = 8
FOUND = 8

EDGES = [[0, 27, 94, 203, 353, 543, 774, 1047, 1360, 1713, 2108, 2544, 3020, 3537, N],
         [0, 448, 1792, N], [0, 448, 1792, N], [0, 1024, N]] + [[0, 1024, N]] * 4 + [[0, N]] * (TILES - 8)
ROOM = [16] + [8] * (TILES - 1)
CHUNKS = [1] + [2] * 7 + [3] * 4 + [2] * (TILES - 12)
NSEG = [len(e) - 1 for e in EDGES]
NCH = [NSEG[t] * CHUNKS[t] for t in range(TILES)]
FILLS = [(c + 1) // 2 for c in NCH]
UNITS = sum(NSEG)
AHEAD = 12
LAG = 9
COUNTING = GROUPS - AHEAD // GROUP


def running(values):
    out = [0]
    for v in values:
        out.append(out[-1] + v)
    return out


KV_AT = [0, NCH[0], 0, NCH[2]] + [NCH[2] + NCH[3], NCH[0], 0, NCH[2]] * (TILES // GROUP - 1)

EARLY = NCH[0] // 4 * 2

U_AT = running(NSEG)
F_AT = running(FILLS)
G_AT = [sum(NCH[i] if i else EARLY for i in range(t % 2, t, 2)) for t in range(TILES + 2)]


class At:

    def __init__(self, g, j, g0):
        self.g = g + j // GROUP if j >= GROUP else g
        self.j = j % GROUP
        self.g0 = g0 + j // GROUP
        self.rep = GROUP * self.g0 + self.j
        self.par = self.rep % 2
        if self.rep < TILES:
            self.nseg, self.room, self.per, self.nch = (NSEG[self.rep], ROOM[self.rep], CHUNKS[self.rep], NCH[self.rep])
            self.fills = FILLS[self.rep]

    @property
    def t(self):
        return self.g * GROUP + self.j

    def total(self, table):
        if isinstance(self.g, int):
            return table[GROUP * self.g + self.j]
        a = GROUP * self.g0 + self.j
        return table[a] + (self.g - self.g0) * (table[a + GROUP] - table[a])

    @property
    def first_fill(self):
        return sum(FILLS[GROUP * self.g0:self.rep])

    def next(self):
        return At(self.g, self.j + 1, self.g0)


def build(nc, x, xT, adj, wqkvT, bq, bk, bqkv, woT, bo, w1T, b1, w2T, b2, g1, be1, g2, be2, out):
    with ExitStack() as ctx:
        def sb(name, shape, dt=F32):
            return ctx.enter_context(nc.sbuf_tensor(name, shape, dt))

        def sem(name):
            return ctx.enter_context(nc.semaphore(name))

        def flat(ap):
            return ap.rearrange("p a b -> p (a b)")

        ps = ctx.enter_context(nc.psum_tensor("ps", [P, BANKS, BANK], F32))
        QE, SMALL, ELL, POST, ME, ACC = 0, 2, 3, 4, 6, 7
        FIRST_BANK, SECOND_BANK = QE, SMALL

        wqkv = sb("wqkv", [P, KC, 3 * D])
        wo = sb("wo", [P, KC, D])
        w1 = sb("w1", [P, KC, FF])
        w2 = sb("w2", [P, FC, D])
        bias_qkv = sb("bias_qkv", [P, 3 * D])
        bias_qT = sb("bias_qT", [P, KC])
        bias_kT = sb("bias_kT", [P, KC])
        bias_1T = sb("bias_1T", [P, FC])
        rows = {n: sb("row_" + n, [P, D]) for n in ("bo", "b2", "g1", "be1", "g2", "be2")}

        ident = sb("ident", [P, P])
        not_ident = sb("not_ident", [P, P])
        before = sb("before", [P, P])
        all_ones = sb("all_ones", [P, P])
        neg_half = sb("neg_half", [P, GROUP])
        eps_col = sb("eps_col", [P, GROUP])
        row_1 = sb("row_1", [P, P])
        edge_no = sb("edge_no", [P, 3 * P])
        edge_col = sb("edge_col", [P, 3])
        slot_no = sb("slot_no", [P, max(ROOM)])
        ones8 = sb("ones8", [P, FOUND], I32)
        holds = sb("holds", [P, UNITS])

        q_all = sb("q_all", [P, TILES, D])
        kv_dram = nc.dram_tensor("kv_table", (N, 2 * D), F32, kind="Internal").ap()
        kv_self = [sb(f"kv_self{i}", [P, 2 * D]) for i in range(2)]

        WORDS = FOUND + 2
        adj_buf = [sb(f"adj_buf{i}", [P, N + FOUND], I32) for i in range(2)]
        counted_out = sb("counted_out", [P, N], mybir.dt.uint8)
        found = sb("found", [P, max(NSEG), max(ROOM)], U32)
        first_idx = sb("first_idx", [P, NSEG[0], ROOM[0] + 2])
        idx_all = sb("idx_all", [P, UNITS - NSEG[0], WORDS])
        counts = sb("counts", [P, UNITS])
        over = sb("over", [P, UNITS])
        neg_mid = sb("neg_mid", [P, UNITS])
        half = sb("half", [P, UNITS])
        bad = sb("bad", [P, 2, UNITS])

        MOST = [max(NCH[i::2]) for i in range(2)]
        REST = max(NCH[1:])
        rt = [sb(f"rt{i}", [P, REST, P]) for i in range(2)]
        onehot = [sb(f"onehot{i}", [P, REST, P]) for i in range(2)]
        spread = sb("spread", [P, REST * FOUND * HEADS])
        slot_hot = [sb(f"slot_hot{i}", [P, MOST[i] * (16 if i == 0 else 8)]) for i in range(2)]
        slot_of = [sb(f"slot_of{i}", [P, MOST[i]]) for i in range(2)]
        row_of = [sb(f"row_of{i}", [P, MOST[i]]) for i in range(2)]
        col_of = [sb(f"col_of{i}", [P, MOST[i]], U32) for i in range(2)]
        picked = sb("picked", [P, REST * FOUND])
        kv_slots = sb("kv_slots", [P, NCH[0] + NCH[1], 2 * D])
        product = [sb(f"product{i}", [P, 2, D]) for i in range(2)]
        s_e = [sb(f"s_e{i}", [P, MOST[i], HEADS]) for i in range(2)]
        s_self = [sb(f"s_self{i}", [P, HEADS]) for i in range(2)]
        absent = sb("absent", [P, max(NSEG[1:]) * FOUND])
        top = sb("top", [P, HEADS])
        top_all = [sb(f"top_all{i}", [P, HEADS]) for i in range(2)]
        below = sb("below", [P, MOST[0] + 1, HEADS])
        spare_dve = sb("spare_dve", [P, GROUP])
        spare_pool = sb("spare_pool", [P, GROUP])
        recip = sb("recip", [P, HEADS])
        flag = sb("flag", [P, 1], I32)
        flag_f = sb("flag_f", [P, 1])

        s_const = sem("s_const")
        s_holds = sem("s_holds")
        HOLDS = len([t for t in range(TILES) if t == 0 or CHUNKS[t] != CHUNKS[t - 1]])
        s_first_weights = sem("s_first_weights")
        s_weights = sem("s_weights")
        s_x = [sem("s_x0"), sem("s_x1")]
        s_x_later = [sem("s_x_later0"), sem("s_x_later1")]
        s_qkv_ps = sem("s_qkv_ps")
        s_qkv_raw = sem("s_qkv_raw")
        s_qkv = sem("s_qkv")
        s_kv_out = [sem("s_kv_out0"), sem("s_kv_out1")]
        adj_loaded = [sem("adj_loaded0"), sem("adj_loaded1")]
        diag_clear = sem("diag_clear")
        counted = sem("counted")
        hunt = sem("hunt")
        extracted = sem("extracted")
        over_ready = sem("over_ready")
        starts_ps = sem("starts_ps")
        starts_link = sem("starts_link")
        starts_ready = sem("starts_ready")
        distance = sem("distance")
        rt_ready = sem("rt_ready")
        lists_ps = sem("lists_ps")
        slots_ready = sem("slots_ready")
        hot_ready = sem("hot_ready")
        picked_ready = sem("picked_ready")
        cols_ready = sem("cols_ready")
        onehot_ready = sem("onehot_ready")
        gathered = [sem("gathered0"), sem("gathered1")]
        gathered_late = sem("gathered_late")
        self_loaded = [sem("self_loaded0"), sem("self_loaded1")]
        qe_ps = sem("qe_ps")
        product_ready = sem("product_ready")
        scores_ready = sem("scores_ready")
        self_product = sem("self_product")
        self_score = sem("self_score")
        spread_ready = sem("spread_ready")
        ell_ps = sem("ell_ps")
        absent_ready = sem("absent_ready")
        ell_masked = sem("ell_masked")
        top_ready = sem("top_ready")
        top_all_ready = sem("top_all_ready")
        me_ps = sem("me_ps")
        below_ready = sem("below_ready")
        probs_ready = sem("probs_ready")
        weighted = sem("weighted")
        acc_ps = sem("acc_ps")
        recip_ready = sem("recip_ready")
        ctx_ready = sem("ctx_ready")
        flag_link = sem("flag_link")
        flag_ready = sem("flag_ready")

        def post_signals(name):
            signals = ("x_loaded x_biased ctxT_ps ctxT_done attn_ps res1 mv1 rstd1 norm h1_done h1T_ps h1T "
                       "ff_ps ff h1_b2 out_ps res2 mv2 rstd2 final stored link plink").split()
            return {n: sem(name + n) for n in signals}

        post_shapes = {
            "ctx": [P, GROUP, D], "ctxT": [P, KC, GROUP * P], "x": [P, GROUP, D], "h1": [P, GROUP, D],
            "ffT": [P, FC, GROUP * P], "stats": [P, GROUP, 6], "mv": [P, GROUP, 2], "rstd": [P, GROUP], "spare": [P, 1],
        }
        x_h1 = sb("post_x_h1", [P, 2, GROUP, D])
        post_buffers = {n: sb("post_" + n, s) for n, s in post_shapes.items() if n not in ("x", "h1")}
        views = {**{n: b[:] for n, b in post_buffers.items()}, "x": x_h1[:, 0], "h1": x_h1[:, 1]}
        post = {"g": GROUP, **views, **post_signals("p_")}

        xbuf = flat(kv_slots[:, 12:16, :]).rearrange("p (b k n) -> p b k n", b=2, k=KC)

        ff_flat = flat(post_buffers["ffT"][:])
        words = NCH[0] * ROOM[0] * HEADS
        spread_of = [ff_flat[:, 0:words], spread[:]]
        rt_of = [ff_flat[:, words:words + NCH[0] * P].rearrange("p (c n) -> p c n", n=P), rt[0][:], rt[1][:]]
        lots = words + NCH[0] * P
        picked_of = [ff_flat[:, lots:lots + NCH[0] * ROOM[0]], picked[:]]
        absent_of = [ff_flat[:, lots + NCH[0] * ROOM[0]:lots + 2 * NCH[0] * ROOM[0]], absent[:]]
        onehot_of = [x_h1[:].rearrange("p a b c -> p (a b c)")[:, 0:NCH[0] * P].rearrange("p (c n) -> p c n", n=P),
                     onehot[0][:], onehot[1][:]]

        def slot_view(first, shape):
            words = shape[0] * shape[1]
            return flat(kv_slots[:, first:first + words // (2 * D), :]).rearrange("p (a b) -> p a b", b=shape[1])

        def half_of(at, ctxT, h1, ffT, signals):
            two = slice(at, at + 2)
            return {"g": 2, "ctx": views["ctx"][:, two, :], "x": views["x"][:, two, :], "stats": views["stats"][:, two, :],
                    "mv": views["mv"][:, two, :], "rstd": views["rstd"][:, two], "spare": views["spare"],
                    "ctxT": slot_view(ctxT, (KC, 2 * P)), "h1": slot_view(h1, (2, D)), "ffT": slot_view(ffT, (FC, 2 * P)),
                    "own_h1": True, **signals}

        first_half = half_of(0, 8, 9, 16, post_signals("h_"))
        second_half = {**half_of(2, 12, 13, 2, {}), **{n: v for n, v in post.items() if n not in views and n != "g"}}
        LAST = GROUPS - 1

        gKT = q_all[:].rearrange("p t d -> p (t d)").rearrange("p (k n) -> p k n", k=KC)
        gmask = flat(kv_slots[:])[:, 0:N]
        gS = adj_buf[1][:, 0:N].bitcast(F32)
        gadj = adj_buf[0][:, 0:N]
        g_xbuf = ff_flat[:, 0:2 * KC * GROUP * P].rearrange("p (b k n) -> p b k n", b=2, k=KC)
        gXT = g_xbuf[:, 0]
        gx = g_xbuf[:, 1, :, 0:P]
        g_small = flat(kv_slots[:])[:, N:]
        gQT = g_small[:, 0:KC * P].rearrange("p (k n) -> p k n", k=KC)
        gPT = g_small[:, KC * P:KC * P + 8 * P]
        gV = g_small[:, KC * P + 8 * P:KC * P + 8 * P + TILES * DK].rearrange("p (t d) -> p t d", d=DK)
        gstat = sb("gstat", [P, 4])
        gpost = {"g": 1, **{n: (v[:, 0:1] if n in ("ctx", "x", "h1", "stats", "mv", "rstd") else v) for n, v in views.items()},
                 **post_signals("g_")}
        gpost["ctxT"] = post_buffers["ctxT"][:, :, 0:P]
        gpost["ffT"] = post_buffers["ffT"][:, :, 0:P]
        (s_gx, s_gkt_ps, s_gkt, s_gadj, s_gmask, s_gdiag, s_gxq, s_gqt_ps, s_gqt, s_gscores, s_gmasked, s_gmax, s_gnm,
         s_gprobs, s_gpt_ps, s_gpt, s_gpv, s_grl, s_gctx, s_gv) = [sem(n) for n in (
            "s_gx s_gkt_ps s_gkt s_gadj s_gmask s_gdiag s_gxq s_gqt_ps s_gqt s_gscores s_gmasked s_gmax s_gnm "
            "s_gprobs s_gpt_ps s_gpt s_gpv s_grl s_gctx s_gv").split()]

        WEIGHT_DMAS = 6 + len(rows)
        CONSTS = 18
        KV_STORES = [GROUPS // 2, GROUPS // 2 - 1 + GROUP]
        PT_TILES = 8
        PT_PARTS = TILES // PT_TILES
        x_rows = x.rearrange("(t p) d -> p t d", p=P)
        out_rows = out.rearrange("(t p) d -> p t d", p=P)
        xT_cols = xT.rearrange("(k p) n -> p k n", p=P)

        def wait(eng, s, value):
            if not isinstance(value, int) or value > 0:
                eng.wait_ge(s, value)


        def unit_range(q):
            return q.total(U_AT)

        def per_unit(table, q, u):
            at = unit_range(q) + u
            return table[:, bass.ds(at, 1)] if not isinstance(at, int) else table[:, at:at + 1]

        def lists(q, u):
            if q.rep == 0:
                return first_idx[:, u, :]
            at = unit_range(q) + u - NSEG[0]
            return flat(idx_all[:, bass.ds(at, 1), :]) if not isinstance(at, int) else idx_all[:, at, :]

        def kv(q):
            return kv_slots[:, KV_AT[q.rep]:KV_AT[q.rep] + q.nch, :]

        def buf(q):
            return 0 if q.rep == 0 else 1 + q.par

        def clear_dve(dve, q):
            a = adj_buf[q.par]
            dve.wait_ge(adj_loaded[q.par], (q.g * 2 + q.j // 2 + 1) * 16)
            diag = a[:, bass.ds(q.t * P, P)] if not isinstance(q.t, int) else a[:, q.t * P:(q.t + 1) * P]
            wait(dve, extracted, q.t)
            nc.vector.tensor_tensor(diag, diag, not_ident[:], ALU.mult).then_inc(diag_clear, 1)

        def extract_dve(dve, q, n):
            a = adj_buf[q.par]
            cols = EDGES[q.rep]
            dve.wait_ge(diag_clear, q.t + 1)
            if not isinstance(q.t, int):
                nc.vector.memset(spare_dve[:, q.j:q.j + 1], 0.0)
            for u in reversed(range(q.nseg)):
                lo, hi = cols[u], cols[u + 1]
                part = a[:, lo:hi + FOUND]
                if hi < N:
                    dve.wait_ge(counted, q.t + 1)
                    nc.vector.memset(a[:, hi:hi + FOUND], 1).then_inc(hunt, 1)
                    n = n + 1
                    dve.wait_ge(hunt, n)
                nc.vector.max_index(found[:, u, 0:FOUND], ones8[:], part).then_inc(hunt, 1)
                n = n + 1
                if q.room > FOUND:
                    dve.wait_ge(counted, q.t + 1)
                    dve.wait_ge(hunt, n)
                    nc.vector.match_replace(part, ones8[:], part, 0.0).then_inc(hunt, 1)
                    dve.wait_ge(hunt, n + 1)
                    nc.vector.memset(a[:, hi:hi + FOUND], 1).then_inc(hunt, 1)
                    dve.wait_ge(hunt, n + 2)
                    nc.vector.max_index(found[:, u, FOUND:2 * FOUND], ones8[:], part).then_inc(hunt, 1)
                    n = n + 3
                dve.wait_ge(hunt, n)
            for u in range(q.nseg):
                last = nc.vector.tensor_scalar(lists(q, u)[:, 0:q.room], found[:, u, 0:q.room], float(cols[u]), None, ALU.add)
            last.then_inc(extracted, 1)

        def hunts(t):
            return sum((1 if h < N else 0) + (4 if ROOM[t] > FOUND else 1) for h in EDGES[t][1:])

        HUNT_AT = running([hunts(t) for t in range(TILES)])

        def count_act(act, q):
            act.wait_ge(diag_clear, q.t + 1)
            wait(act, counted, q.t)
            for u in range(q.nseg):
                lo, hi = EDGES[q.rep][u], EDGES[q.rep][u + 1]
                last = nc.scalar.activation(counted_out[:, lo:hi], adj_buf[q.par][:, lo:hi], ACT.Copy,
                                            accum_out=per_unit(counts, q, u))
            last.then_inc(counted, 1)

        def units_of(table, g, g0):
            a, b = At(g, 0, g0), At(g, GROUP, g0)
            n = sum(NSEG[GROUP * g0:GROUP * g0 + GROUP])
            at = a.total(U_AT)
            return (table[:, bass.ds(at, n)] if not isinstance(at, int) else table[:, at:at + n]), n

        def starts_over(dve, g, g0):
            dve.wait_ge(counted, (g + 1) * GROUP)
            if g0 == 0:
                n0 = NSEG[0]
                nc.vector.tensor_scalar(over[:, 0:n0], counts[:, 0:n0], float(ROOM[0]), None, ALU.is_gt)
                n = U_AT[GROUP]
                nc.vector.tensor_scalar(over[:, n0:n], counts[:, n0:n], float(FOUND), None, ALU.is_gt).then_inc(over_ready, 1)
            else:
                c, n = units_of(counts, g, g0)
                nc.vector.tensor_scalar(units_of(over, g, g0)[0], c, float(FOUND), None, ALU.is_gt).then_inc(over_ready, 1)

        def starts_pe(pe, g, g0):
            c, n = units_of(counts, g, g0)
            pe.wait_ge(over_ready, g + 1)
            wait(pe, starts_ready, g)
            if isinstance(g, int):
                pe.wait_ge(counted, (g + 1) * GROUP)
            nc.tensor.matmul(ps[:, SMALL, 0:n], before[:], c, start=True, stop=True)
            nc.tensor.matmul(ps[:, SMALL, n:2 * n], all_ones[:], c, start=True, stop=True)
            nc.tensor.matmul(ps[:, SMALL, 2 * n:3 * n], all_ones[:], units_of(over, g, g0)[0], start=True, stop=True).then_inc(starts_ps, 1)

        def starts_dve(dve, g, g0):
            c, n = units_of(counts, g, g0)
            mid = units_of(neg_mid, g, g0)[0]
            small = ps[:, SMALL, :]
            nc.vector.tensor_scalar(mid, c, -0.5, 0.5, ALU.mult, ALU.add).then_inc(starts_link, 1)
            nc.vector.tensor_scalar(units_of(half, g, g0)[0], c, 0.5, -0.25, ALU.mult, ALU.add)
            dve.wait_ge(starts_ps, g + 1)
            dve.wait_ge(starts_link, g + 1)
            nc.vector.tensor_tensor(mid, mid, small[:, 0:n], ALU.subtract)
            at = At(g, 0, g0).total(U_AT)
            if g0 == 0:
                nc.vector.tensor_copy(first_idx[:, :, ROOM[0]], small[:, 0:NSEG[0]])
                nc.vector.tensor_copy(idx_all[:, 0:n - NSEG[0], FOUND], small[:, NSEG[0]:n])
                nc.vector.tensor_tensor(bad[:, 0, 0:n], small[:, n:2 * n], holds[:, 0:n], ALU.is_gt)
                nc.vector.tensor_copy(bad[:, 1, 0:n], small[:, 2 * n:3 * n]).then_inc(starts_ready, 1)
            else:
                there = bass.ds(at - NSEG[0], n) if not isinstance(at, int) else slice(at - NSEG[0], at - NSEG[0] + n)
                here = bass.ds(at, n) if not isinstance(at, int) else slice(at, at + n)
                nc.vector.tensor_copy(idx_all[:, there, FOUND], small[:, 0:n])
                nc.vector.tensor_tensor(bad[:, 0, here], small[:, n:2 * n], holds[:, here], ALU.is_gt)
                nc.vector.tensor_copy(bad[:, 1, here], small[:, 2 * n:3 * n]).then_inc(starts_ready, 1)

        def distance_act(act, q):
            wait(act, me_ps, q.t - 1)
            act.wait_ge(starts_ready, q.g + 1)
            for u in range(q.nseg):
                w = q.per * P
                last = nc.scalar.activation(flat(rt_of[buf(q)])[:, u * w:(u + 1) * w], edge_no[:, 0:w], ACT.Abs,
                                            bias=per_unit(neg_mid, q, u))
            last.then_inc(distance, 1)

        def rt_dve(dve, q):
            dve.wait_ge(distance, q.t + 1)
            for u in range(q.nseg):
                w = q.per * P
                part = flat(rt_of[buf(q)])[:, u * w:(u + 1) * w]
                last = nc.vector.tensor_scalar(part, part, per_unit(half, q, u), None, ALU.is_le)
            last.then_inc(rt_ready, 1)

        def lists_pe(pe, q, prefixes):
            pe.wait_ge(rt_ready, q.t + 1)
            pe.wait_ge(starts_ready, prefixes)
            wait(pe, onehot_ready, q.t)
            w = q.room + 2
            for c in range(q.nch):
                last = nc.tensor.matmul(ps[:, SMALL, c * w:(c + 1) * w], rt_of[buf(q)][:, c, :], lists(q, c // q.per),
                                        start=True, stop=True)
            last.then_inc(lists_ps, 1)

        def hot(q):
            return slot_hot[q.par][:, 0:q.nch * q.room].rearrange("p (c k) -> p c k", k=q.room)

        def cols_dve(dve, q):
            w = q.room + 2
            at = ps[:, SMALL, 0:q.nch * w].rearrange("p (c w) -> p c w", w=w)
            dve.wait_ge(lists_ps, q.t + 1)
            slots = slot_of[q.par][:, 0:q.nch]
            nc.vector.tensor_tensor(slots.rearrange("p (u c) -> p u c", c=q.per),
                                    edge_col[:, 0:q.per].unsqueeze(1).to_broadcast([P, q.nseg, q.per]),
                                    at[:, :, q.room].rearrange("p (u c) -> p u c", c=q.per), ALU.subtract).then_inc(slots_ready, 1)
            nc.vector.tensor_copy(row_of[q.par][:, 0:q.nch], at[:, :, q.room + 1])
            dve.wait_ge(slots_ready, q.t + 1)
            nc.vector.tensor_tensor(hot(q), slot_no[:, 0:q.room].unsqueeze(1).to_broadcast([P, q.nch, q.room]),
                                    slots.unsqueeze(2).to_broadcast([P, q.nch, q.room]), ALU.is_equal).then_inc(hot_ready, 1)
            dve.wait_ge(hot_ready, q.t + 1)
            wait(dve, cols_ready, q.t)
            pick = picked_of[min(q.rep, 1)][:, 0:q.nch * q.room].rearrange("p (c k) -> p c k", k=q.room)
            nc.vector.tensor_tensor(pick, hot(q), at[:, :, 0:q.room], ALU.mult).then_inc(picked_ready, 1)
            dve.wait_ge(picked_ready, q.t + 1)
            with nc.allow_low_precision(reason="one whole number below 4096 and zeros"):
                nc.vector.tensor_reduce(col_of[q.par][:, 0:q.nch], pick, AX_X, ALU.add).then_inc(cols_ready, 1)

        def onehot_dve(dve, q):
            wait(dve, acc_ps, q.t - 1)
            for c in range(q.nch):
                last = nc.vector.tensor_scalar(onehot_of[buf(q)][:, c, :], row_1[:], row_of[q.par][:, c:c + 1], None, ALU.is_equal)
            last.then_inc(onehot_ready, 1)

        def gather_pool(pool, q):
            pool.wait_ge(cols_ready, q.t + 1)
            if q.rep in (2, 3):
                pool.wait_ge(acc_ps, 1)
            else:
                wait(pool, acc_ps, q.t - 3)
            if not isinstance(q.t, int):
                nc.gpsimd.tensor_tensor(spare_pool[:, q.j:q.j + 1], eps_col[:, 0:1], eps_col[:, 0:1], ALU.add)
            for c in range(q.nch):
                nc.gpsimd.indirect_dma_start(kv(q)[:, c, :], None, kv_dram,
                                             bass.IndirectOffsetOnAxis(ap=col_of[q.par][:, c:c + 1], axis=0)
                                             ).then_inc(gathered[q.par] if q.rep or c < EARLY else gathered_late, 16)

        def self_load(act, q):
            wait(act, acc_ps, q.t - 1)
            rows_at = bass.ds(q.t * P, P) if not isinstance(q.t, int) else slice(q.t * P, (q.t + 1) * P)
            act.dma_start(kv_self[q.par][:], kv_dram[rows_at, :]).then_inc(self_loaded[q.par], 16)

        def q_tile(q):
            return q_all[:, bass.ds(q.t, 1), :] if not isinstance(q.t, int) else q_all[:, q.t:q.t + 1, :]

        def fills(q):
            for f in range(q.fills):
                place = q.first_fill + f
                yield QE + place % 2, 2 * f, min(2, q.nch - 2 * f), place, q.total(F_AT) + f

        def spread_queries_pe(pe, q):
            for i, (bank, c0, n, place, number) in enumerate(fills(q)):
                wait(pe, product_ready, number if place == 0 else number - 1)
                for c in range(n):
                    last = nc.tensor.matmul(ps[:, bank, c * D:(c + 1) * D], rt_of[buf(q)][:, c0 + c, :], flat(q_tile(q)),
                                            start=True, stop=True)
                last.then_inc(qe_ps, 1)

        def scores_dve(dve, q):
            dve.wait_ge(gathered[q.par], (q.total(G_AT) + (q.nch if q.rep else EARLY)) * 16)
            for bank, c0, n, place, number in fills(q):
                if q.rep == 0 and c0 == EARLY:
                    dve.wait_ge(gathered_late, (q.nch - EARLY) * 16)
                dve.wait_ge(qe_ps, number + 1)
                wait(dve, scores_ready, number if place == 0 else number - 1)
                nc.vector.tensor_tensor(product[place % 2][:, 0:n, :], ps[:, bank, 0:n * D].rearrange("p (c d) -> p c d", d=D),
                                        kv(q)[:, c0:c0 + n, 0:D], ALU.mult).then_inc(product_ready, 1)
                dve.wait_ge(product_ready, number + 1)
                if c0 == 0:
                    wait(dve, below_ready, q.t - 1)
                nc.vector.tensor_reduce(s_e[q.par][:, c0:c0 + n, :].rearrange("p c h -> p (c h)"),
                                        product[place % 2][:, 0:n, :].rearrange("p c (h d) -> p (c h) d", d=DK), AX_X, ALU.add
                                        ).then_inc(scores_ready, 1)

        def self_dve(dve, q):
            dve.wait_ge(self_loaded[q.par], (q.g * 2 + q.j // 2 + 1) * 16)
            keys = kv_self[q.par][:, 0:D]
            nc.vector.tensor_tensor(keys.unsqueeze(1), q_tile(q), keys.unsqueeze(1), ALU.mult).then_inc(self_product, 1)
            dve.wait_ge(self_product, q.t + 1)
            nc.vector.tensor_reduce(s_self[q.par][:], keys.rearrange("p (h d) -> p h d", d=DK), AX_X, ALU.add).then_inc(self_score, 1)

        def spread_dve(dve, q):
            dve.wait_ge(scores_ready, q.total(F_AT) + q.fills)
            w = q.room * HEADS
            dst = spread_of[min(q.rep, 1)][:, 0:q.nch * w].rearrange("p (c k h) -> p c k h", k=q.room, h=HEADS)
            nc.vector.tensor_tensor(dst, hot(q).unsqueeze(3).to_broadcast([P, q.nch, q.room, HEADS]),
                                    s_e[q.par][:, 0:q.nch, :].unsqueeze(2).to_broadcast([P, q.nch, q.room, HEADS]), ALU.mult
                                    ).then_inc(spread_ready, 1)

        def ell_pe(pe, q):
            pe.wait_ge(spread_ready, q.t + 1)
            pe.wait_ge(onehot_ready, q.t + 1)
            w = q.room * HEADS
            for u in range(q.nseg):
                for c in range(q.per):
                    k = u * q.per + c
                    bank, off = ELL + u * w // BANK, u * w % BANK
                    last = nc.tensor.matmul(ps[:, bank, off:off + w], onehot_of[buf(q)][:, k, :],
                                            spread_of[min(q.rep, 1)][:, k * w:(k + 1) * w], start=(c == 0), stop=(c == q.per - 1))
            last.then_inc(ell_ps, 1)

        def top_dve(dve, q):
            wait(dve, ell_masked, q.t)
            for u in range(q.nseg):
                last = nc.vector.tensor_scalar(absent_of[min(q.rep, 1)][:, u * q.room:(u + 1) * q.room], slot_no[:, 0:q.room],
                                               per_unit(counts, q, u), MISSING, ALU.is_ge, ALU.mult)
            last.then_inc(absent_ready, 1)
            dve.wait_ge(absent_ready, q.t + 1)
            dve.wait_ge(ell_ps, q.t + 1)
            k = q.nseg * q.room
            masked = spread_of[min(q.rep, 1)][:, 0:k * HEADS]
            src = flat(ps[:, ELL:ELL + (k * HEADS + BANK - 1) // BANK, :])[:, 0:k * HEADS]
            nc.vector.tensor_tensor(masked.rearrange("p (k h) -> p k h", h=HEADS), src.rearrange("p (k h) -> p k h", h=HEADS),
                                    absent_of[min(q.rep, 1)][:, 0:k].unsqueeze(2).to_broadcast([P, k, HEADS]), ALU.add).then_inc(ell_masked, 1)
            dve.wait_ge(ell_masked, q.t + 1)
            nc.vector.tensor_reduce(top[:], masked.rearrange("p (k h) -> p h k", h=HEADS), AX_X, ALU.max).then_inc(top_ready, 1)
            dve.wait_ge(top_ready, q.t + 1)
            nc.vector.tensor_tensor(top_all[q.par][:], top[:], s_self[q.par][:], ALU.max).then_inc(top_all_ready, 1)

        def me_pe(pe, q):
            pe.wait_ge(top_all_ready, q.t + 1)
            for c in range(q.nch):
                last = nc.tensor.matmul(ps[:, ME, c * HEADS:(c + 1) * HEADS], rt_of[buf(q)][:, c, :], top_all[q.par][:], start=True, stop=True)
            last.then_inc(me_ps, 1)

        def below_dve(dve, q):
            dve.wait_ge(me_ps, q.t + 1)
            nc.vector.tensor_tensor(below[:, q.nch, :], s_self[q.par][:], top_all[q.par][:], ALU.subtract)
            nc.vector.tensor_tensor(flat(below[:, 0:q.nch, :]), flat(s_e[q.par][:, 0:q.nch, :]), ps[:, ME, 0:q.nch * HEADS], ALU.subtract
                                    ).then_inc(below_ready, 1)

        def probs_act(act, q):
            act.wait_ge(below_ready, q.t + 1)
            nc.scalar.activation(kv(q)[:, :, D - HEADS:D], below[:, 0:q.nch, :], ACT.Exp, scale=SCALE)
            nc.scalar.activation(kv_self[q.par][:, D - HEADS:D], below[:, q.nch, :], ACT.Exp, scale=SCALE).then_inc(probs_ready, 1)

        def weight_dve(dve, q):
            dve.wait_ge(probs_ready, q.t + 1)
            for v, p, n in ((kv(q)[:, :, D:2 * D], kv(q)[:, :, D - HEADS:D], q.nch),
                            (kv_self[q.par][:, D:2 * D].unsqueeze(1), kv_self[q.par][:, D - HEADS:D].unsqueeze(1), 1)):
                v = v.rearrange("p c (h d) -> p c h d", d=DK)
                last = nc.vector.tensor_tensor(v, v, p.unsqueeze(3).to_broadcast([P, n, HEADS, DK]), ALU.mult)
            last.then_inc(weighted, 1)

        def sum_pe(pe, q):
            pe.wait_ge(weighted, q.t + 1)
            wait(pe, ctx_ready, q.t)
            w = slice(D - HEADS, 2 * D)
            for c in range(q.nch):
                nc.tensor.matmul(ps[:, ACC, 0:D + HEADS], onehot_of[buf(q)][:, c, :], kv(q)[:, c, w], start=(c == 0), stop=False)
            nc.tensor.matmul(ps[:, ACC, 0:D + HEADS], ident[:], kv_self[q.par][:, w], start=False, stop=True).then_inc(acc_ps, 1)

        def ctx_dve(dve, q):
            dve.wait_ge(acc_ps, q.t + 1)
            wait(dve, ctx_ready, q.t)
            nc.vector.reciprocal(recip[:], ps[:, ACC, 0:HEADS]).then_inc(recip_ready, 1)
            dve.wait_ge(recip_ready, q.t + 1)
            if q.j == 0:
                wait(dve, post["ctxT_ps"], q.g)
            nc.vector.tensor_tensor(post["ctx"][:, q.j, :].rearrange("p (h d) -> p h d", d=DK),
                                    ps[:, ACC, HEADS:HEADS + D].rearrange("p (h d) -> p h d", d=DK),
                                    recip[:].unsqueeze(2).to_broadcast([P, HEADS, DK]), ALU.mult).then_inc(ctx_ready, 1)


        def post_load(sp, q, n, t):
            sp.dma_start(q["x"], x_rows[:, bass.ds(t, q["g"]), :] if not isinstance(t, int) else x_rows[:, t:t + q["g"], :]
                         ).then_inc(q["x_loaded"], 16)

        def post_store(sp, q, n, t):
            sp.wait_ge(q["final"], n + 1)
            sp.dma_start(out_rows[:, bass.ds(t, q["g"]), :] if not isinstance(t, int) else out_rows[:, t:t + q["g"], :], q["h1"]
                         ).then_inc(q["stored"], 16)

        def transposed(pe, src, g, bank, done):
            for k in range(KC):
                for j in range(g):
                    c = (k * g + j) * P
                    last = nc.tensor.transpose(ps[:, bank + c // BANK, c % BANK:c % BANK + P], src[:, j, k * P:(k + 1) * P], ident[:])
            last.then_inc(done, 1)

        def post_pe_ctx(pe, q, n, bank, ctx_sem, ctx_value):
            pe.wait_ge(ctx_sem, ctx_value)
            wait(pe, q["res2"], n)
            transposed(pe, q["ctx"], q["g"], bank, q["ctxT_ps"])

        def post_pe_attn(pe, q, n, bank):
            pe.wait_ge(q["ctxT_done"], n + 1)
            for j in range(q["g"]):
                for k in range(KC):
                    last = nc.tensor.matmul(ps[:, bank + j * D // BANK, j * D % BANK:j * D % BANK + D],
                                            q["ctxT"][:, k, j * P:(j + 1) * P], wo[:, k, :], start=(k == 0), stop=(k == KC - 1))
            last.then_inc(q["attn_ps"], 1)

        def post_pe_h1(pe, q, n, bank):
            pe.wait_ge(q["h1_done"], n + 1)
            transposed(pe, q["h1"], q["g"], bank, q["h1T_ps"])

        def post_pe_ff(pe, q, n, bank, fs):
            for f in fs:
                if f == 0:
                    pe.wait_ge(q["h1T"], n + 1)
                if f >= 2:
                    pe.wait_ge(q["ff"], n * FC + f - 1)
                for k in range(KC):
                    last = nc.tensor.matmul(ps[:, bank + f % 2, 0:q["g"] * P], w1[:, k, f * P:(f + 1) * P], q["ctxT"][:, k, :],
                                            start=(k == 0), stop=(k == KC - 1))
                last.then_inc(q["ff_ps"], 1)

        def post_pe_out(pe, q, n, bank, js):
            for j in js:
                if j == 0:
                    pe.wait_ge(q["ff"], (n + 1) * FC)
                for f in range(FC):
                    last = nc.tensor.matmul(ps[:, bank + j * D // BANK, j * D % BANK:j * D % BANK + D],
                                            q["ffT"][:, f, j * P:(j + 1) * P], w2[:, f, :], start=(f == 0), stop=(f == FC - 1))
                if j == q["g"] - 1:
                    last.then_inc(q["out_ps"], 1)

        def post_act_copy(act, q, n, bank, ready, done):
            w = KC * q["g"] * P
            act.wait_ge(q[ready], n + 1)
            src = flat(ps[:, bank:bank + (w + BANK - 1) // BANK, :])[:, 0:w]
            nc.scalar.copy(q["ctxT"], src.rearrange("p (k n) -> p k n", k=KC)).then_inc(q[done], 1)

        def post_act_ff(act, q, n, bank, fs):
            for f in fs:
                act.wait_ge(q["ff_ps"], n * FC + f + 1)
                nc.scalar.activation(q["ffT"][:, f, :], ps[:, bank + f % 2, 0:q["g"] * P], ACT.Relu,
                                     bias=bias_1T[:, f:f + 1]).then_inc(q["ff"], 1)

        def post_dve_sum(dve, q, n, bank, k):
            g = q["g"]
            w = g * D
            src = flat(ps[:, bank:bank + (w + BANK - 1) // BANK, :])[:, 0:w]
            ps_ready, other, add, res, mv_done = ((q["attn_ps"], q["x_biased"], q["x"], q["res1"], q["mv1"]) if k == 0 else
                                                  (q["out_ps"], q["h1_b2"], q["h1"], q["res2"], q["mv2"]))
            dve.wait_ge(ps_ready, n + 1)
            dve.wait_ge(other, n + 1)
            if k == 0 and "own_h1" not in q:
                wait(dve, q["stored"], n * 16)
            nc.vector.tensor_tensor(flat(q["h1"]), src, flat(add), ALU.add).then_inc(res, 1)
            dve.wait_ge(res, n + 1)
            for j in range(g):
                last = nc.vector.bn_stats(q["stats"][:, j, :], q["h1"][:, j, :])
            last.then_inc(q["link"], 1)
            dve.wait_ge(q["link"], n * 2 + 1 + k)
            nc.vector.memset(q["spare"], 0.0)
            for j in range(g):
                last = nc.vector.bn_aggr(q["mv"][:, j, :], q["stats"][:, j, :])
            last.then_inc(mv_done, 1)

        def post_dve_norm(dve, q, n, k):
            dve.wait_ge(q["rstd2" if k else "rstd1"], n + 1)
            scale, shift = (rows["g2"], rows["be2"]) if k else (rows["g1"], rows["be1"])
            for j in range(q["g"]):
                h = q["h1"][:, j, :]
                last = nc.vector.scalar_tensor_tensor(h, h, q["mv"][:, j, 0:1], scale[:], ALU.subtract, ALU.mult)
            last.then_inc(q["norm"], 1)
            dve.wait_ge(q["norm"], n * 2 + 1 + k)
            for j in range(q["g"]):
                h = q["h1"][:, j, :]
                last = nc.vector.scalar_tensor_tensor(h, h, q["rstd"][:, j:j + 1], shift[:], ALU.mult, ALU.add)
            last.then_inc(q["final" if k else "h1_done"], 1)

        def wide(name, g):
            return rows[name][:].unsqueeze(1).to_broadcast([P, g, D])

        def post_pool_bias(pool, q, n):
            pool.wait_ge(q["x_loaded"], (n + 1) * 16)
            nc.gpsimd.tensor_tensor(q["x"], q["x"], wide("bo", q["g"]), ALU.add).then_inc(q["x_biased"], 1)

        def post_pool_rstd(pool, q, n, k):
            g = q["g"]
            pool.wait_ge(q["mv2" if k else "mv1"], n + 1)
            nc.gpsimd.tensor_tensor(q["rstd"], q["mv"][:, :, 1], eps_col[:, 0:g], ALU.add).then_inc(q["plink"], 1)
            pool.wait_ge(q["plink"], n * 2 + k + 1)
            nc.gpsimd.tensor_tensor(q["rstd"], q["rstd"], neg_half[:, 0:g], ALU.pow).then_inc(q["rstd2" if k else "rstd1"], 1)

        def post_pool_b2(pool, q, n):
            pool.wait_ge(q["h1T_ps"], n + 1)
            nc.gpsimd.tensor_tensor(q["h1"], q["h1"], wide("b2", q["g"]), ALU.add).then_inc(q["h1_b2"], 1)


        def general_sync(sp):
            with sp.Fori(0, GROUPS) as c:
                sp.wait_ge(s_gkt, c * KC)
                sp.dma_start(gXT, xT_cols[:, :, bass.ds(c * GROUP * P, GROUP * P)]).then_inc(s_gx, 16)
            with sp.Fori(0, TILES) as t:
                sp.wait_ge(s_gqt_ps, t)
                sp.dma_start(gx, xT_cols[:, :, bass.ds(t * P, P)]).then_inc(s_gxq, 16)
                sp.wait_ge(s_gmask, t)
                sp.dma_start(gadj, adj[bass.ds(t * P, P), :]).then_inc(s_gadj, 16)
                for h in range(HEADS):
                    sp.wait_ge(s_gpv, t * HEADS + h)
                    sp.dma_start(gV, kv_dram.rearrange("(t p) d -> p t d", p=P)[:, :, D + h * DK:D + (h + 1) * DK]).then_inc(s_gv, 16)
                post_load(sp, gpost, t, t)
                post_store(sp, gpost, t, t)
            sp.wait_ge(gpost["stored"], TILES * 16)

        def general_pool(pool):
            with pool.Fori(0, TILES) as t:
                post_pool_bias(pool, gpost, t)
                post_pool_rstd(pool, gpost, t, 0)
                post_pool_b2(pool, gpost, t)
                post_pool_rstd(pool, gpost, t, 1)

        def general_act(act):
            with act.Fori(0, GROUPS) as c:
                for part in range(KC):
                    act.wait_ge(s_gkt_ps, c * KC + part + 1)
                    nc.scalar.activation(gKT[:, part, bass.ds(c * GROUP * P, GROUP * P)], ps[:, part, :], ACT.Identity,
                                         bias=bias_kT[:, part:part + 1]).then_inc(s_gkt, 1)
            with act.Fori(0, TILES) as t:
                act.wait_ge(s_gqt_ps, t + 1)
                for part in range(KC):
                    last = nc.scalar.activation(gQT[:, part, :], ps[:, 0, part * P:(part + 1) * P], ACT.Identity,
                                                bias=bias_qT[:, part:part + 1])
                last.then_inc(s_gqt, 1)
                for h in range(HEADS):
                    n = t * HEADS + h
                    act.wait_ge(s_gnm, n + 1)
                    nc.scalar.activation(gS, gS, ACT.Exp, bias=gstat[:, 1:2], scale=SCALE,
                                         accum_out=gstat[:, 2:3]).then_inc(s_gprobs, 1)
                    for part in range(PT_PARTS):
                        act.wait_ge(s_gpt_ps, n * PT_PARTS + part + 1)
                        nc.scalar.copy(gPT, flat(ps[:, 0:PT_TILES * P // BANK, :])).then_inc(s_gpt, 1)
                post_act_copy(act, gpost, t, 0, "ctxT_ps", "ctxT_done")
                post_act_copy(act, gpost, t, 0, "h1T_ps", "h1T")
                post_act_ff(act, gpost, t, 0, range(FC))

        def general_pe(pe):
            with pe.Fori(0, GROUPS) as c:
                pe.wait_ge(s_gx, (c + 1) * 16)
                pe.wait_ge(s_gkt, c * KC)
                for part in range(KC):
                    for k in range(KC):
                        last = nc.tensor.matmul(ps[:, part, :], wqkv[:, k, D + part * P:D + (part + 1) * P], gXT[:, k, :],
                                                start=(k == 0), stop=(k == KC - 1))
                    last.then_inc(s_gkt_ps, 1)
            pe.wait_ge(s_gkt, GROUPS * KC)
            with pe.Fori(0, TILES) as t:
                pe.wait_ge(gpost["res2"], t)
                pe.wait_ge(s_gxq, (t + 1) * 16)
                for part in range(KC):
                    for k in range(KC):
                        last = nc.tensor.matmul(ps[:, 0, part * P:(part + 1) * P], wqkv[:, k, part * P:(part + 1) * P],
                                                gx[:, k, :], start=(k == 0), stop=(k == KC - 1))
                last.then_inc(s_gqt_ps, 1)
                pe.wait_ge(s_gqt, t + 1)
                for h in range(HEADS):
                    n = t * HEADS + h
                    at = DK * (h % 4)
                    pe.wait_ge(s_gctx, n)
                    for c in range(BANKS):
                        last = nc.tensor.matmul(ps[:, c, :], gQT[at:at + DK, h // 4, :],
                                                gKT[at:at + DK, h // 4, c * BANK:(c + 1) * BANK], start=True, stop=True)
                    last.then_inc(s_gscores, 1)
                    pe.wait_ge(s_gv, (n + 1) * 16)
                    pe.wait_ge(s_gprobs, n + 1)
                    for part in range(PT_PARTS):
                        for j in range(PT_TILES):
                            c = j * P
                            k = part * PT_TILES + j
                            last = nc.tensor.transpose(ps[:, c // BANK, c % BANK:c % BANK + P], gS[:, k * P:(k + 1) * P], ident[:])
                        last.then_inc(s_gpt_ps, 1)
                        pe.wait_ge(s_gpt, n * PT_PARTS + part + 1)
                        for j in range(PT_TILES):
                            k = part * PT_TILES + j
                            last = nc.tensor.matmul(ps[:, BANKS - 1, 0:DK], gPT[:, j * P:(j + 1) * P], gV[:, k, :],
                                                    start=(k == 0), stop=(k == TILES - 1))
                    last.then_inc(s_gpv, 1)
                post_pe_ctx(pe, gpost, t, 0, s_gctx, (t + 1) * HEADS)
                post_pe_attn(pe, gpost, t, 0)
                post_pe_h1(pe, gpost, t, 0)
                post_pe_ff(pe, gpost, t, 0, range(FC))
                post_pe_out(pe, gpost, t, 0, range(1))

        def general_dve(dve):
            with dve.Fori(0, TILES) as t:
                dve.wait_ge(s_gadj, (t + 1) * 16)
                nc.vector.tensor_tensor(gadj[:, bass.ds(t * P, P)], gadj[:, bass.ds(t * P, P)], ident[:], ALU.add).then_inc(s_gdiag, 1)
                dve.wait_ge(s_gdiag, t + 1)
                nc.vector.tensor_scalar(gmask, gadj, 0.0, NEG, ALU.is_equal, ALU.mult).then_inc(s_gmask, 1)
                dve.wait_ge(s_gmask, t + 1)
                for h in range(HEADS):
                    n = t * HEADS + h
                    dve.wait_ge(s_gscores, n + 1)
                    nc.vector.tensor_tensor(gS, flat(ps[:]), gmask, ALU.add).then_inc(s_gmasked, 1)
                    dve.wait_ge(s_gmasked, n + 1)
                    nc.vector.tensor_reduce(gstat[:, 0:1], gS, AX_X, ALU.max).then_inc(s_gmax, 1)
                    dve.wait_ge(s_gmax, n + 1)
                    nc.vector.tensor_scalar(gstat[:, 1:2], gstat[:, 0:1], -SCALE, None, ALU.mult).then_inc(s_gnm, 1)
                    dve.wait_ge(s_gprobs, n + 1)
                    nc.vector.reciprocal(gstat[:, 3:4], gstat[:, 2:3]).then_inc(s_grl, 1)
                    dve.wait_ge(s_grl, n + 1)
                    dve.wait_ge(s_gpv, n + 1)
                    nc.vector.tensor_scalar(gpost["ctx"][:, 0, h * DK:(h + 1) * DK], ps[:, BANKS - 1, 0:DK], gstat[:, 3:4], None,
                                            ALU.mult).then_inc(s_gctx, 1)
                post_dve_sum(dve, gpost, t, 0, 0)
                post_dve_norm(dve, gpost, t, 0)
                post_dve_sum(dve, gpost, t, 0, 1)
                post_dve_norm(dve, gpost, t, 1)

        def general(eng, path):
            eng.wait_ge(flag_ready, 1)
            eng.wait_ge(post["stored"], GROUPS * 16)
            eng.wait_ge(first_half["stored"], 16)
            raised = eng.value_load(flag[0:1, 0:1], min_val=0, max_val=1)
            with eng.If(raised > 0):
                path(eng)
            eng.wait_ge(flag_ready, 1)


        def loops(eng, group):
            for g in range(3):
                group(g, g)
            with eng.Fori(3, COUNTING) as g:
                group(g, 3)
            with eng.Fori(COUNTING, GROUPS - 1) as g:
                group(g, COUNTING)
            group(GROUPS - 1, GROUPS - 1)

        def searched(g, j, g0):
            steps = {1: (0,), 2: (1,), 3: (2, 3)}
            return [At(g, i + AHEAD, g0) for i in steps.get(j, ())] if g0 < COUNTING else []

        block = ctx.enter_context(nc.Block())

        @block.sync
        def _(sp):
            def load_adj(q):
                wait(sp, extracted, q.t - 1)
                wait(sp, counted, q.t - 1)
                rows_at = bass.ds(q.t * P, P) if not isinstance(q.t, int) else slice(q.t * P, (q.t + 1) * P)
                sp.dma_start(adj_buf[q.par][:, 0:N], adj[rows_at, :]).then_inc(adj_loaded[q.par], 16)

            def load_x(c):
                sp.dma_start(xbuf[:, c], xT_cols[:, :, c * GROUP * P:(c + 1) * GROUP * P]).then_inc(s_x[c], 16)

            load_adj(At(0, 0, 0))
            load_x(0)
            load_x(1)
            for t in range(1, AHEAD):
                load_adj(At(t // GROUP, t % GROUP, t // GROUP))
            with sp.Fori(AHEAD // GROUP, GROUPS) as g:
                for j in range(GROUP):
                    load_adj(At(g, j, AHEAD // GROUP))
            general(sp, general_sync)

        @block.gpsimd
        def _(pool):
            for t, v in ((ident, 0.0), (neg_half, -0.5), (eps_col, EPS), (not_ident, 1.0), (before, 1.0), (all_ones, 1.0),
                         (ones8, 1)):
                nc.gpsimd.memset(t[:], v).then_inc(s_const, 1)
            for b in adj_buf:
                nc.gpsimd.memset(b[:, N:N + FOUND], 1).then_inc(s_const, 1)
            pool.wait_ge(s_const, 9)
            diagonal = [[-1, P]]
            nc.gpsimd.affine_select(out=ident[:], in_=ident[:], compare_op=ALU.not_equal, fill=1.0, base=0,
                                    pattern=diagonal, channel_multiplier=1).then_inc(s_const, 1)
            nc.gpsimd.affine_select(out=not_ident[:], in_=not_ident[:], compare_op=ALU.not_equal, fill=0.0, base=0,
                                    pattern=diagonal, channel_multiplier=1).then_inc(s_const, 1)
            nc.gpsimd.affine_select(out=before[:], in_=before[:], compare_op=ALU.is_gt, fill=0.0, base=0,
                                    pattern=[[1, P]], channel_multiplier=-1).then_inc(s_const, 1)
            exact = {"allow_small_or_imprecise_dtypes": True}
            nc.gpsimd.iota(row_1[:], [[1, P]], base=1, channel_multiplier=0, **exact).then_inc(s_const, 1)
            nc.gpsimd.iota(edge_no[:], [[1, 3 * P]], base=0, channel_multiplier=0, **exact).then_inc(s_const, 1)
            nc.gpsimd.iota(edge_col[:], [[P, 3]], base=0, channel_multiplier=1, **exact).then_inc(s_const, 1)
            nc.gpsimd.iota(slot_no[:], [[1, max(ROOM)]], base=0, channel_multiplier=0, **exact).then_inc(s_const, 1)
            nc.gpsimd.iota(first_idx[:, :, ROOM[0] + 1], [[0, NSEG[0]]], base=1, channel_multiplier=1, **exact).then_inc(s_const, 1)
            nc.gpsimd.iota(idx_all[:, :, FOUND + 1], [[0, UNITS - NSEG[0]]], base=1, channel_multiplier=1, **exact).then_inc(s_const, 1)
            u = 0
            while u < UNITS:
                t = [i for i in range(TILES) if U_AT[i] <= u < U_AT[i + 1]][0]
                end = t
                while end < TILES and CHUNKS[end] == CHUNKS[t]:
                    end += 1
                nc.gpsimd.memset(holds[:, u:U_AT[end]], float(CHUNKS[t] * P)).then_inc(s_holds, 1)
                u = U_AT[end]
            pool.wait_ge(s_first_weights, 2 * 16)

            kv_groups = kv_dram.rearrange("(t p) d -> p t d", p=P)

            def project_pair(i, last):
                for half_no in range(2):
                    first = (i * 2 + half_no) * GROUP
                    for r in range(GROUP):
                        t = first + r
                        pool.wait_ge(s_qkv_raw, t + 1)
                        q_at = q_all[:, bass.ds(t, 1), :] if not isinstance(t, int) else q_all[:, t:t + 1, :]
                        nc.gpsimd.tensor_tensor(q_at, q_at, bias_qkv[:, 0:D].unsqueeze(1), ALU.add)
                        kv_at = kv_slots[:, half_no * GROUP + r, :]
                        nc.gpsimd.tensor_tensor(kv_at, kv_at, bias_qkv[:, D:3 * D], ALU.add).then_inc(s_qkv, 1)
                        if last and half_no == 1:
                            pool.wait_ge(s_qkv, t + 1)
                            pool.dma_start(kv_groups[:, t, :], kv_at).then_inc(s_kv_out[1], 16)
                    if not last:
                        cols = first * P + 2 * GROUP * P
                        pool.dma_start(xbuf[:, half_no], xT_cols[:, :, bass.ds(cols, GROUP * P)]).then_inc(s_x_later[half_no], 16)
                    if last and half_no == 1:
                        continue
                    pool.wait_ge(s_qkv, first + GROUP)
                    there = bass.ds(first, GROUP) if not isinstance(first, int) else slice(first, first + GROUP)
                    pool.dma_start(kv_groups[:, there, :], kv_slots[:, half_no * GROUP:(half_no + 1) * GROUP, :]
                                   ).then_inc(s_kv_out[half_no], 16)

            with pool.Fori(0, GROUPS // 2 - 1) as i:
                project_pair(i, False)
            project_pair(GROUPS // 2 - 1, True)
            for half_no in range(2):
                pool.wait_ge(s_kv_out[half_no], KV_STORES[half_no] * 16)
            gather_pool(pool, At(0, 0, 0))
            gather_pool(pool, At(0, 1, 0))

            def group(g, g0):
                n = g - 1
                for j in range(GROUP):
                    q = At(g, j, g0)
                    if j == 0 and g0 > 1:
                        post_pool_rstd(pool, post, n - 1, 1)
                    if j == 1 and g0 > 0:
                        post_pool_rstd(pool, post, n, 0)
                    if q.rep + 2 < TILES:
                        gather_pool(pool, q.next().next())
                    if j == 0 and g0 > 0:
                        post_pool_bias(pool, post, n)
                    if j == 2 and g0 > 0:
                        post_pool_b2(pool, post, n)
                    if j == 3 and g0 == LAST:
                        post_pool_bias(pool, first_half, 0)
                        post_pool_bias(pool, second_half, LAST)
                        post_pool_rstd(pool, first_half, 0, 0)

            loops(pool, group)
            post_pool_rstd(pool, post, LAST - 1, 1)
            post_pool_b2(pool, first_half, 0)
            post_pool_rstd(pool, second_half, LAST, 0)
            post_pool_b2(pool, second_half, LAST)
            post_pool_rstd(pool, first_half, 0, 1)
            post_pool_rstd(pool, second_half, LAST, 1)
            general(pool, general_pool)

        @block.scalar
        def _(act):
            for dst, src in ((wqkv, wqkvT.rearrange("(k p) n -> p k n", p=P)), (bias_qkv, bqkv.to_broadcast([P, 3 * D]))):
                act.dma_start(dst[:], src).then_inc(s_first_weights, 16)
            count_act(act, At(0, 0, 0))
            for dst, src in ((wo, woT.rearrange("(k p) n -> p k n", p=P)),
                             (w1, w1T.rearrange("(k p) n -> p k n", p=P)), (w2, w2T.rearrange("(k p) n -> p k n", p=P)),
                             (bias_qT, bq), (bias_kT, bk), (bias_1T, b1)):
                act.dma_start(dst[:], src).then_inc(s_weights, 16)
            for name, src in (("bo", bo), ("b2", b2), ("g1", g1), ("be1", be1), ("g2", g2), ("be2", be2)):
                act.dma_start(rows[name][:], src.to_broadcast([P, D])).then_inc(s_weights, 16)

            def take(t):
                c = t // GROUP
                act.wait_ge(s_qkv_ps, t + 1)
                wait(act, s_kv_out[c % 2], c // 2 * 16)
                bank = 6 * (t % 2)
                nc.scalar.copy(kv_slots[:, t % (2 * GROUP), :], ps[:, bank, :])
                nc.scalar.copy(q_all[:, t, :], ps[:, bank + 1, 0:D]).then_inc(s_qkv_raw, 1)

            known = 2 * GROUP * (GROUPS // 2 - 1)
            for t in range(TILES):
                take(t)
                if t + 1 in (known, known + 1):
                    distance_act(act, At(0, t + 1 - known, 0))
                elif t >= LAG and (t - LAG) % 2 == 0:
                    i = (t - LAG) // 2 + (1 if t < known else 0)
                    count_act(act, At(i // GROUP, i % GROUP, i // GROUP))
            for half_no in range(2):
                act.wait_ge(s_kv_out[half_no], KV_STORES[half_no] * 16)
            self_load(act, At(0, 0, 0))
            self_load(act, At(0, 1, 0))
            distance_act(act, At(0, 2, 0))

            def group(g, g0):
                n = g - 1
                for j in range(GROUP):
                    q = At(g, j, g0)
                    later = g0 > 0
                    probs_act(act, q)
                    if later and j == 3:
                        post_act_ff(act, post, n, POST, range(5, FC))
                    if later and j == 2:
                        post_act_ff(act, post, n, POST, range(0, 2))
                    for found_in in searched(g, j, g0):
                        count_act(act, found_in)
                    if later and j == 0:
                        post_act_copy(act, post, n, POST, "ctxT_ps", "ctxT_done")
                    if later and j == 1:
                        post_act_copy(act, post, n, POST, "h1T_ps", "h1T")
                    if later and j == 2:
                        post_act_ff(act, post, n, POST, range(2, 5))
                    if q.rep + 2 < TILES:
                        self_load(act, q.next().next())
                    if q.rep + 3 < TILES:
                        distance_act(act, q.next().next().next())
                    if j == 0 and g0 > 1:
                        post_store(act, post, n - 1, (n - 1) * GROUP)
                    if g0 == LAST and j == 3:
                        post_act_copy(act, first_half, 0, FIRST_BANK, "ctxT_ps", "ctxT_done")
                    if j == 2:
                        wait(act, post["res1"], g)
                        act.wait_ge(acc_ps, 1)
                        if g0 == LAST:
                            post_load(act, first_half, 0, TILES - 4)
                            post_load(act, second_half, LAST, TILES - 2)
                        else:
                            post_load(act, post, g, g * GROUP)

            loops(act, group)
            post_act_copy(act, first_half, 0, FIRST_BANK, "h1T_ps", "h1T")
            post_act_copy(act, second_half, LAST, SECOND_BANK, "ctxT_ps", "ctxT_done")
            post_store(act, post, LAST - 1, (LAST - 1) * GROUP)
            post_act_ff(act, first_half, 0, FIRST_BANK, range(FC))
            post_act_copy(act, second_half, LAST, SECOND_BANK, "h1T_ps", "h1T")
            post_act_ff(act, second_half, LAST, SECOND_BANK, range(FC))
            post_store(act, first_half, 0, TILES - 4)
            post_store(act, second_half, LAST, TILES - 2)
            general(act, general_act)

        @block.tensor
        def _(pe):
            pe.wait_ge(s_first_weights, 2 * 16)

            def project(i):
                for half_no in range(2):
                    if isinstance(i, int) and i == 0:
                        pe.wait_ge(s_x[half_no], 16)
                    else:
                        pe.wait_ge(s_x_later[half_no], i * 16)
                    for r in range(GROUP):
                        bank = 6 * (r % 2)
                        wait(pe, s_qkv_raw, (i * 2 + half_no) * GROUP + r - 1)
                        for at, cols in ((bank, slice(D, 3 * D)), (bank + 1, slice(0, D))):
                            for k in range(KC):
                                last = nc.tensor.matmul(ps[:, at, 0:cols.stop - cols.start], xbuf[:, half_no, k, r * P:(r + 1) * P],
                                                        wqkv[:, k, cols], start=(k == 0), stop=(k == KC - 1))
                        last.then_inc(s_qkv_ps, 1)

            project(0)
            with pe.Fori(1, GROUPS // 2 - 1) as i:
                project(i)
            pe.wait_ge(s_const, CONSTS)
            for g in range(2):
                starts_pe(pe, g, g)
            project(GROUPS // 2 - 1)
            t0, t1 = At(0, 0, 0), At(0, 1, 0)
            lists_pe(pe, t0, 2)
            pe.wait_ge(onehot_ready, 1)
            starts_pe(pe, 2, 2)
            lists_pe(pe, t1, 3)
            pe.wait_ge(s_qkv, TILES)
            pe.wait_ge(s_weights, 16 * WEIGHT_DMAS)
            spread_queries_pe(pe, t0)
            ell_pe(pe, t0)
            me_pe(pe, t0)
            spread_queries_pe(pe, t1)

            def group(g, g0):
                n = g - 1
                for j in range(GROUP):
                    q = At(g, j, g0)
                    later = g0 > 0
                    if q.rep + 2 < TILES:
                        lists_pe(pe, q.next().next(), g + 3 if g0 < COUNTING else GROUPS)
                    if q.rep + 1 < TILES:
                        ell_pe(pe, q.next())
                    if later and j == 3:
                        post_pe_ff(pe, post, n, POST, range(FC - 1, FC))
                    if later and j == 0:
                        post_pe_ctx(pe, post, n, POST, ctx_ready, g * GROUP)
                    if q.rep + 2 < TILES and FILLS[q.rep + 2] <= 2:
                        spread_queries_pe(pe, q.next().next())
                    if later and j == 0:
                        post_pe_attn(pe, post, n, POST)
                    if later and j == 2:
                        post_pe_ff(pe, post, n, POST, range(2, 4))
                    if g0 == LAST and j == 3:
                        post_pe_ctx(pe, first_half, 0, FIRST_BANK, ctx_ready, TILES - 2)
                    if later and j == 3:
                        post_pe_out(pe, post, n, POST, range(0, 1))
                    if g0 == LAST and j == 3:
                        post_pe_attn(pe, first_half, 0, FIRST_BANK)
                    sum_pe(pe, q)
                    if later and j == 1:
                        post_pe_h1(pe, post, n, POST)
                    if later and j == 2:
                        post_pe_ff(pe, post, n, POST, range(4, 5))
                    if later and j == 3:
                        post_pe_out(pe, post, n, POST, range(1, 2))
                    if q.rep + 1 < TILES:
                        me_pe(pe, q.next())
                    if q.rep + 2 < TILES and FILLS[q.rep + 2] > 2:
                        spread_queries_pe(pe, q.next().next())
                    if later and j == 1:
                        post_pe_ff(pe, post, n, POST, range(0, 2))
                    if later and j == 2:
                        post_pe_ff(pe, post, n, POST, range(5, FC - 1))
                    if later and j == 3:
                        post_pe_out(pe, post, n, POST, range(2, 3))
                    if g0 < COUNTING and j == 3:
                        starts_pe(pe, g + 3, g0 + 3)
                    if later and j == 3:
                        post_pe_out(pe, post, n, POST, range(3, 4))

            loops(pe, group)
            post_pe_h1(pe, first_half, 0, FIRST_BANK)
            post_pe_ctx(pe, second_half, LAST, SECOND_BANK, ctx_ready, TILES)
            post_pe_ff(pe, first_half, 0, FIRST_BANK, range(0, 2))
            post_pe_attn(pe, second_half, LAST, SECOND_BANK)
            post_pe_ff(pe, first_half, 0, FIRST_BANK, range(2, FC))
            post_pe_h1(pe, second_half, LAST, SECOND_BANK)
            post_pe_ff(pe, second_half, LAST, SECOND_BANK, range(FC))
            post_pe_out(pe, first_half, 0, FIRST_BANK, range(2))
            post_pe_out(pe, second_half, LAST, SECOND_BANK, range(2))
            general(pe, general_pe)

        @block.vector
        def _(dve):
            dve.wait_ge(s_const, CONSTS)
            dve.wait_ge(s_holds, HOLDS)

            def extract(q):
                extract_dve(dve, q, q.total(HUNT_AT))

            def search(g, js=range(GROUP)):
                for j in js:
                    clear_dve(dve, At(g, j, g))
                    extract(At(g, j, g))
                if GROUP - 1 in js:
                    starts_over(dve, g, g)

            search(0)
            search(1)
            starts_dve(dve, 0, 0)
            starts_dve(dve, 1, 1)
            t0, t1 = At(0, 0, 0), At(0, 1, 0)
            rt_dve(dve, t0)
            rt_dve(dve, t1)
            search(2, range(3))
            cols_dve(dve, t0)
            onehot_dve(dve, t0)
            search(2, [3])
            starts_dve(dve, 2, 2)
            cols_dve(dve, t1)
            onehot_dve(dve, t1)
            scores_dve(dve, t0)
            self_dve(dve, t0)
            spread_dve(dve, t0)
            top_dve(dve, t0)

            def group(g, g0):
                n = g - 1
                for j in range(GROUP):
                    q = At(g, j, g0)
                    later = g0 > 0
                    q1, q2 = q.next(), q.next().next()
                    if q1.rep < TILES:
                        scores_dve(dve, q1)
                    if q2.rep < TILES:
                        rt_dve(dve, q2)
                    below_dve(dve, q)
                    if q1.rep < TILES:
                        spread_dve(dve, q1)
                    if later and j == 1:
                        post_dve_sum(dve, post, n, POST, 0)
                    if g0 > 1 and j == 0:
                        post_dve_sum(dve, post, n - 1, POST, 1)
                    for found_in in searched(g, j, g0)[:1]:
                        clear_dve(dve, found_in)
                    if q2.rep < TILES:
                        cols_dve(dve, q2)
                    weight_dve(dve, q)
                    if later and j == 1:
                        post_dve_norm(dve, post, n, 0)
                    if q1.rep < TILES:
                        self_dve(dve, q1)
                        top_dve(dve, q1)
                    if g0 > 1 and j == 0:
                        post_dve_norm(dve, post, n - 1, 1)
                    for i, found_in in enumerate(searched(g, j, g0)):
                        if i > 0:
                            clear_dve(dve, found_in)
                        extract(found_in)
                    if g0 == LAST and j == 3:
                        post_dve_sum(dve, first_half, 0, FIRST_BANK, 0)
                    ctx_dve(dve, q)
                    if q2.rep < TILES:
                        onehot_dve(dve, q2)
                if g0 < COUNTING:
                    starts_over(dve, g + 3, g0 + 3)
                    starts_dve(dve, g + 3, g0 + 3)

            loops(dve, group)
            post_dve_norm(dve, first_half, 0, 0)
            for q, n, bank, k in ((post, LAST - 1, POST, 1), (second_half, LAST, SECOND_BANK, 0), (first_half, 0, FIRST_BANK, 1),
                                  (second_half, LAST, SECOND_BANK, 1)):
                post_dve_sum(dve, q, n, bank, k)
                post_dve_norm(dve, q, n, k)
            nc.vector.tensor_reduce(flag_f[:], flat(bad[:]), AX_X, ALU.max).then_inc(flag_link, 1)
            dve.wait_ge(flag_link, 1)
            nc.vector.tensor_scalar(flag[:], flag_f[:], 0.0, None, ALU.is_gt).then_inc(flag_ready, 1)
            general(dve, general_dve)


def kernel(**inputs):
    import numpy as _np
    import concourse.bacc as _bacc
    from concourse import mybir as _mybir
    from concourse.bass_utils import run_bass_kernel_spmd as _run

    w = {k.replace("L0_gnn_", ""): _np.ascontiguousarray(v) for k, v in inputs.items()}
    arrays = {
        "x": w["x"],
        "xT": _np.ascontiguousarray(w["x"].T),
        "adj": w["adj"],
        "wqkvT": _np.ascontiguousarray(_np.concatenate([w["Wq"], w["Wk"], w["Wv"]]).T),
        "bq": _np.ascontiguousarray(w["bq"].reshape(-1, 128).T),
        "bk": _np.ascontiguousarray(w["bk"].reshape(-1, 128).T),
        "bqkv": _np.concatenate([w["bq"], w["bk"], w["bv"]]).reshape(1, -1),
        "woT": _np.ascontiguousarray(w["Wo"].T),
        "bo": w["bo"].reshape(1, -1),
        "w1T": _np.ascontiguousarray(w["W1"].T),
        "b1": _np.ascontiguousarray(w["b1"].reshape(-1, 128).T),
        "w2T": _np.ascontiguousarray(w["W2"].T),
        "b2": w["b2"].reshape(1, -1),
        "g1": w["ln1_g"].reshape(1, -1),
        "be1": w["ln1_b"].reshape(1, -1),
        "g2": w["ln2_g"].reshape(1, -1),
        "be2": w["ln2_b"].reshape(1, -1),
    }
    nc = _bacc.Bacc("TRN2", target_bir_lowering=False, num_devices=1)
    args = [nc.dram_tensor(f"in_{n}", a.shape, _mybir.dt.from_np(a.dtype), kind="ExternalInput").ap() for n, a in arrays.items()]
    args.append(nc.dram_tensor("out_dram", (4096, 256), _mybir.dt.float32, kind="ExternalOutput").ap())
    build(nc, *args)
    r = _run(nc, [{f"in_{n}": a for n, a in arrays.items()}], core_ids=[0])
    return r.results[0]["out_dram"]
```
